# Optimizing a Trainium2 kernel written in Bass

```python
import numpy as np
import jax
import jax.numpy as jnp

def _softmax(x, axis=-1):
    return jax.nn.softmax(x, axis=axis)

def _gelu(x):
    return jax.nn.gelu(x, approximate=True)

def _silu(x):
    return jax.nn.silu(x)

def _sigmoid(x):
    return jax.nn.sigmoid(x)

def _layernorm(x, axis=-1, eps=1e-05):
    m = jnp.mean(x, axis=axis, keepdims=True)
    v = jnp.var(x, axis=axis, keepdims=True)
    return (x - m) / jnp.sqrt(v + eps)

def _scatter_add(tgt, idx, src, axis=0):
    return tgt.at[idx].add(src)

def _segment_sum(src, seg, n):
    return jax.ops.segment_sum(src, seg, n)
kernel_name = 'mk_perceiver_d1_seqx_r2_a373e8'

def setup_inputs(seed: int=0):
    np.random.seed(seed)
    _w = jnp.asarray

    def _rec_inputs():
        import jax
        import jax.numpy as jnp
        _rk = jax.random.key(seed)
        x = 0.0002417 + 0.9998 * jax.random.normal(jax.random.fold_in(_rk, 1), (8, 64, 512), jnp.float32)
        _lenS = 64 - jax.random.randint(jax.random.fold_in(_rk, 7), (8,), 0, max(1, 64 // 4) + 1, jnp.int32)
        _lenS2 = 1601 - jax.random.randint(jax.random.fold_in(_rk, 8), (8,), 0, max(1, 1601 // 4) + 1, jnp.int32)
        _ctx_1024P = jax.random.normal(jax.random.fold_in(_rk, 11), (8, 16, 512), jnp.float32)
        _ctx_1024c = jax.random.dirichlet(jax.random.fold_in(_rk, 511), 0.3 * jnp.ones((16,), jnp.float32), (8, 1601))
        _ctx_1024t = jnp.einsum('bsk,bkd->bsd', _ctx_1024c, _ctx_1024P)
        _ctx_1024t = _ctx_1024t * jax.lax.rsqrt(jnp.mean(jnp.square(_ctx_1024t)) + 1e-12) * 0.953939
        ctx_1024 = 7.22013e-05 + 1.00017 * (_ctx_1024t + 0.3 * jax.random.normal(jax.random.fold_in(_rk, 611), (8, 1601, 512), jnp.float32))
        _validS = jnp.arange(64)[None, :] < _lenS[:, None]
        _validS2 = jnp.arange(1601)[None, :] < _lenS2[:, None]
        _causal = jnp.tril(jnp.ones((64, 64), dtype=bool))
        mask_BxS2_if0 = jnp.where(jnp.ones((8, 1601), dtype=bool), 0, 1).astype(jnp.int32)
        return (x, ctx_1024, mask_BxS2_if0)
    x, ctx_1024, mask_BxS2_if0 = _rec_inputs()

    def _L0_xattn_setup():
        import jax, jax.numpy as jnp
        import numpy as np
        import math
        B, M, D, H, NK = (4, 1024, 512, 16, 5)
        HD = D // H

        def _gather_pad0(x, idx):
            Bx, Hx, W, hd = x.shape
            valid = (idx >= 0) & (idx < W)
            idxc = jnp.clip(idx, 0, W - 1).reshape(Bx, Hx, -1)
            g = jnp.take_along_axis(x, idxc[..., None], axis=2)
            g = g.reshape(idx.shape + (hd,))
            return g * valid[..., None].astype(x.dtype)
        key = jax.random.key(seed)
        ks = jax.random.split(key, 9)
        w = lambda k, shape: jax.random.normal(k, shape, jnp.float32) * 0.02
        return {'k': jax.random.normal(ks[0], (B, M, D), jnp.float32), 'v': jax.random.normal(ks[1], (B, M, D), jnp.float32), 'q': jax.random.normal(ks[2], (B, M, D), jnp.float32), 'mask': jnp.zeros((B, M), jnp.int32), 'Wk': w(ks[3], (D, D)), 'bk': jnp.zeros((D,), jnp.float32), 'Wv': w(ks[4], (D, D)), 'bv': jnp.zeros((D,), jnp.float32), 'Wq': w(ks[5], (D, D)), 'bq': jnp.zeros((D,), jnp.float32), 'Woff': w(ks[6], (H * NK, D)), 'boff': jnp.zeros((H * NK,), jnp.float32), 'Wo': w(ks[7], (D, D)), 'bo': jnp.zeros((D,), jnp.float32)}
    _L0_xattn_all = _L0_xattn_setup()
    _L0_xattn_in = {k: v for k, v in _L0_xattn_all.items() if k in ('Wk', 'bk', 'Wv', 'bv', 'Wq', 'bq', 'Woff', 'boff', 'Wo', 'bo')}
    del _L0_xattn_all

    def _L0_attn_setup():
        import jax, jax.numpy as jnp
        import numpy as np
        INPUT_SIZE = 512
        STATE_SIZE = 512
        OUTPUT_SIZE = 512
        key = jax.random.key(seed)
        ks = jax.random.split(key, 8)
        B, T = (8, 1024)
        u = jax.random.normal(ks[0], (B, T, INPUT_SIZE), dtype=jnp.float32)
        log_A = jax.random.normal(ks[1], (STATE_SIZE,), dtype=jnp.float32) * 0.5
        sB = 1.0 / np.sqrt(INPUT_SIZE)
        sC = 1.0 / np.sqrt(STATE_SIZE)
        sD = 1.0 / np.sqrt(INPUT_SIZE)
        W_B = jax.random.uniform(ks[2], (STATE_SIZE, INPUT_SIZE), jnp.float32, -sB, sB)
        b_B = jax.random.uniform(ks[3], (STATE_SIZE,), jnp.float32, -sB, sB)
        W_C = jax.random.uniform(ks[4], (OUTPUT_SIZE, STATE_SIZE), jnp.float32, -sC, sC)
        b_C = jax.random.uniform(ks[5], (OUTPUT_SIZE,), jnp.float32, -sC, sC)
        W_D = jax.random.uniform(ks[6], (OUTPUT_SIZE, INPUT_SIZE), jnp.float32, -sD, sD)
        b_D = jax.random.uniform(ks[7], (OUTPUT_SIZE,), jnp.float32, -sD, sD)
        log_dt = jnp.full((1,), -1.0, dtype=jnp.float32)
        return {'u': u, 'log_A': log_A, 'W_B': W_B, 'b_B': b_B, 'W_C': W_C, 'b_C': b_C, 'W_D': W_D, 'b_D': b_D, 'log_dt': log_dt}
    _L0_attn_all = _L0_attn_setup()
    _L0_attn_in = {k: v for k, v in _L0_attn_all.items() if k in ('log_A', 'W_B', 'b_B', 'W_C', 'b_C', 'W_D', 'b_D', 'log_dt')}
    del _L0_attn_all

    def _L0_ffn_setup():
        import jax, jax.numpy as jnp
        import numpy as np
        from jax import lax
        TOP_K = 4
        N_GROUP = 4
        TOPK_GROUP = 2
        ROUTED_SCALE = 2.5
        NEG_INF = -1000000000.0

        def _route(xf, router_weight, router_bias):
            T = xf.shape[0]
            E = router_weight.shape[0]
            logits = xf @ router_weight.T
            scores = jax.nn.sigmoid(logits)
            s_choice = scores + router_bias
            per_group = E // N_GROUP
            sg = s_choice.reshape(T, N_GROUP, per_group)
            group_scores = lax.top_k(sg, 2)[0].sum(-1)
            _, gidx = lax.top_k(group_scores, TOPK_GROUP)
            gmask = jnp.zeros((T, N_GROUP), dtype=bool).at[jnp.arange(T)[:, None], gidx].set(True)
            masked = jnp.where(gmask[:, :, None], sg, NEG_INF).reshape(T, E)
            _, topk_idx = lax.top_k(masked, TOP_K)
            w = jnp.take_along_axis(scores, topk_idx, axis=1)
            w = w / (w.sum(-1, keepdims=True) + 1e-20) * ROUTED_SCALE
            combine = jnp.zeros((T, E), dtype=xf.dtype).at[jnp.arange(T)[:, None], topk_idx].add(w)
            return combine
        key = jax.random.key(seed)
        ks = jax.random.split(key, 6)
        B, S, H, I, E = (2, 1024, 512, 256, 16)
        x = jax.random.normal(ks[0], (B, S, H), dtype=jnp.float32)
        router_weight = jax.random.normal(ks[1], (E, H), dtype=jnp.float32) * 0.02
        router_bias = jnp.zeros((E,), dtype=jnp.float32)
        w_gate = jax.random.normal(ks[2], (E, I, H), dtype=jnp.float32) * 0.02
        w_up = jax.random.normal(ks[3], (E, I, H), dtype=jnp.float32) * 0.02
        w_down = jax.random.normal(ks[4], (E, H, I), dtype=jnp.float32) * 0.02
        return {'x': x, 'router_weight': router_weight, 'router_bias': router_bias, 'w_gate': w_gate, 'w_up': w_up, 'w_down': w_down}
    _L0_ffn_all = _L0_ffn_setup()
    _L0_ffn_in = {k: v for k, v in _L0_ffn_all.items() if k in ('router_weight', 'router_bias', 'w_gate', 'w_up', 'w_down')}
    del _L0_ffn_all
    return {'x': x, 'ctx_1024': ctx_1024, 'mask_BxS2_if0': mask_BxS2_if0, 'L0_xattn_Wk': _L0_xattn_in['Wk'], 'L0_xattn_bk': _L0_xattn_in['bk'], 'L0_xattn_Wv': _L0_xattn_in['Wv'], 'L0_xattn_bv': _L0_xattn_in['bv'], 'L0_xattn_Wq': _L0_xattn_in['Wq'], 'L0_xattn_bq': _L0_xattn_in['bq'], 'L0_xattn_Woff': _L0_xattn_in['Woff'], 'L0_xattn_boff': _L0_xattn_in['boff'], 'L0_xattn_Wo': _L0_xattn_in['Wo'], 'L0_xattn_bo': _L0_xattn_in['bo'], 'L0_attn_log_A': _L0_attn_in['log_A'], 'L0_attn_W_B': _L0_attn_in['W_B'], 'L0_attn_b_B': _L0_attn_in['b_B'], 'L0_attn_W_C': _L0_attn_in['W_C'], 'L0_attn_b_C': _L0_attn_in['b_C'], 'L0_attn_W_D': _L0_attn_in['W_D'], 'L0_attn_b_D': _L0_attn_in['b_D'], 'L0_attn_log_dt': _L0_attn_in['log_dt'], 'L0_ffn_router_weight': _L0_ffn_in['router_weight'], 'L0_ffn_router_bias': _L0_ffn_in['router_bias'], 'L0_ffn_w_gate': _L0_ffn_in['w_gate'], 'L0_ffn_w_up': _L0_ffn_in['w_up'], 'L0_ffn_w_down': _L0_ffn_in['w_down']}

def reference(x, ctx_1024, mask_BxS2_if0, L0_xattn_Wk, L0_xattn_bk, L0_xattn_Wv, L0_xattn_bv, L0_xattn_Wq, L0_xattn_bq, L0_xattn_Woff, L0_xattn_boff, L0_xattn_Wo, L0_xattn_bo, L0_attn_log_A, L0_attn_W_B, L0_attn_b_B, L0_attn_W_C, L0_attn_b_C, L0_attn_W_D, L0_attn_b_D, L0_attn_log_dt, L0_ffn_router_weight, L0_ffn_router_bias, L0_ffn_w_gate, L0_ffn_w_up, L0_ffn_w_down):
    import jax
    import jax.numpy as jnp

    def _L0_xattn_ref(k, v, q, mask, Wk, bk, Wv, bv, Wq, bq, Woff, boff, Wo, bo):
        import jax, jax.numpy as jnp
        import numpy as np
        import math
        B, M, D, H, NK = (4, 1024, 512, 16, 5)
        HD = D // H

        def _gather_pad0(x, idx):
            Bx, Hx, W, hd = x.shape
            valid = (idx >= 0) & (idx < W)
            idxc = jnp.clip(idx, 0, W - 1).reshape(Bx, Hx, -1)
            g = jnp.take_along_axis(x, idxc[..., None], axis=2)
            g = g.reshape(idx.shape + (hd,))
            return g * valid[..., None].astype(x.dtype)
        Bq, Q, _ = q.shape
        key_len = k.shape[1]
        K = jnp.einsum('bmd,ed->bme', k, Wk) + bk
        V = jnp.einsum('bmd,ed->bme', v, Wv) + bv
        Qp = jnp.einsum('bqd,ed->bqe', q, Wq) + bq
        off = jnp.einsum('bqd,ed->bqe', Qp, Woff) + boff
        off = off.reshape(Bq, Q, H, NK).transpose(0, 2, 1, 3)
        Kh = K.reshape(Bq, key_len, H, HD).transpose(0, 2, 1, 3)
        Vh = V.reshape(Bq, key_len, H, HD).transpose(0, 2, 1, 3)
        Qh = Qp.reshape(Bq, Q, H, HD).transpose(0, 2, 1, 3)
        loc = jnp.arange(Q, dtype=jnp.float32)[:, None]
        left = -NK // 2
        ref = jnp.arange(left, NK + left, dtype=jnp.float32)
        sign_lens = (1 - mask).sum(-1).astype(jnp.float32) - 1.0
        loc_x = jnp.mod(ref + off + loc, sign_lens[:, None, None, None])
        xg = loc_x / (key_len - 1) * 2.0 - 1.0
        ix = ((xg + 1.0) * key_len - 1.0) / 2.0
        x0 = jnp.floor(ix)
        dx = ix - x0
        i0 = x0.astype(jnp.int32)
        i1 = i0 + 1
        w0 = (1.0 - dx)[..., None]
        w1 = dx[..., None]
        sk = 0.5 * (w0 * _gather_pad0(Kh, i0) + w1 * _gather_pad0(Kh, i1))
        sv = 0.5 * (w0 * _gather_pad0(Vh, i0) + w1 * _gather_pad0(Vh, i1))
        scores = jnp.einsum('bhqd,bhqkd->bhqk', Qh / math.sqrt(HD), sk)
        attn = jax.nn.softmax(scores, axis=-1)
        ctx = jnp.einsum('bhqk,bhqkd->bhqd', attn, sv)
        ctx = ctx.transpose(0, 2, 1, 3).reshape(Bq, Q, H * HD)
        return jnp.einsum('bqd,ed->bqe', ctx, Wo) + bo

    def _L0_attn_ref(u, log_A, W_B, b_B, W_C, b_C, W_D, b_D, log_dt):
        import jax, jax.numpy as jnp
        import numpy as np
        INPUT_SIZE = 512
        STATE_SIZE = 512
        OUTPUT_SIZE = 512
        dt = jnp.exp(log_dt)
        A = -jnp.exp(log_A)
        A_bar = jnp.exp(A * dt)
        Bu = (jnp.einsum('bti,ni->btn', u, W_B) + b_B) * dt
        Bu_t = jnp.swapaxes(Bu, 0, 1)

        def step(x, bu):
            x = A_bar * x + bu
            return (x, x)
        x0 = jnp.zeros((u.shape[0], A_bar.shape[0]), dtype=u.dtype)
        _, xs = jax.lax.scan(step, x0, Bu_t)
        xs = jnp.swapaxes(xs, 0, 1)
        y = jnp.einsum('btn,on->bto', xs, W_C) + b_C + jnp.einsum('bti,oi->bto', u, W_D) + b_D
        return y

    def _L0_ffn_ref(x, router_weight, router_bias, w_gate, w_up, w_down):
        import jax, jax.numpy as jnp
        import numpy as np
        from jax import lax
        TOP_K = 4
        N_GROUP = 4
        TOPK_GROUP = 2
        ROUTED_SCALE = 2.5
        NEG_INF = -1000000000.0

        def _route(xf, router_weight, router_bias):
            T = xf.shape[0]
            E = router_weight.shape[0]
            logits = xf @ router_weight.T
            scores = jax.nn.sigmoid(logits)
            s_choice = scores + router_bias
            per_group = E // N_GROUP
            sg = s_choice.reshape(T, N_GROUP, per_group)
            group_scores = lax.top_k(sg, 2)[0].sum(-1)
            _, gidx = lax.top_k(group_scores, TOPK_GROUP)
            gmask = jnp.zeros((T, N_GROUP), dtype=bool).at[jnp.arange(T)[:, None], gidx].set(True)
            masked = jnp.where(gmask[:, :, None], sg, NEG_INF).reshape(T, E)
            _, topk_idx = lax.top_k(masked, TOP_K)
            w = jnp.take_along_axis(scores, topk_idx, axis=1)
            w = w / (w.sum(-1, keepdims=True) + 1e-20) * ROUTED_SCALE
            combine = jnp.zeros((T, E), dtype=xf.dtype).at[jnp.arange(T)[:, None], topk_idx].add(w)
            return combine
        B, S, H = x.shape
        E = w_gate.shape[0]
        xf = x.reshape(-1, H)
        combine = _route(xf, router_weight, router_bias)
        out = jnp.zeros_like(xf)
        for e in range(E):
            g = xf @ w_gate[e].T
            u = xf @ w_up[e].T
            y_e = jax.nn.silu(g) * u @ w_down[e].T
            out = out + combine[:, e:e + 1] * y_e
        return out.reshape(B, S, H)
    x = x + _L0_xattn_ref(ctx_1024, ctx_1024, _layernorm(x, axis=-1), mask_BxS2_if0, L0_xattn_Wk, L0_xattn_bk, L0_xattn_Wv, L0_xattn_bv, L0_xattn_Wq, L0_xattn_bq, L0_xattn_Woff, L0_xattn_boff, L0_xattn_Wo, L0_xattn_bo)
    x = x + _L0_attn_ref(_layernorm(x, axis=-1), L0_attn_log_A, L0_attn_W_B, L0_attn_b_B, L0_attn_W_C, L0_attn_b_C, L0_attn_W_D, L0_attn_b_D, L0_attn_log_dt)
    x = x + _L0_ffn_ref(_layernorm(x, axis=-1), L0_ffn_router_weight, L0_ffn_router_bias, L0_ffn_w_gate, L0_ffn_w_up, L0_ffn_w_down)
    return x

_drawn_inputs = setup_inputs


def setup_inputs(seed=0):
    import zlib

    import numpy as np

    out = dict(_drawn_inputs(seed))
    spreads = {'L0_xattn_bk': (0.0, 0.8),
     'L0_xattn_bv': (0.0, 0.312),
     'L0_xattn_bq': (0.0, 0.8),
     'L0_xattn_boff': (0.0, 0.8),
     'L0_xattn_bo': (0.0, 0.1),
     'L0_ffn_router_bias': (0.0, 0.28)}
    factors = {'L0_xattn_Wk': 8.0, 'L0_xattn_Wq': 4.787, 'L0_xattn_Woff': 4.716, 'L0_attn_b_B': 3.097}
    for name, (base, spread) in spreads.items():
        noise = np.random.default_rng([zlib.crc32(name.encode()), seed]).standard_normal(out[name].shape)
        drawn = base * np.exp(spread * noise) if base else spread * noise
        out[name] = jnp.asarray(drawn.astype(out[name].dtype))
    for name, factor in factors.items():
        out[name] = (out[name] * factor).astype(out[name].dtype)
    return out
```

```python
from contextlib import ExitStack

import numpy as np

import concourse.bass as bass
from concourse import mybir

P = 128
B, S, D, M = 8, 64, 512, 1601
T = B * S
NT = T // P
KC = D // P
H, NK = 16, 5
HD = D // H
NB = 13
DEAD = 32
E, I = 16, 256
EPS = 1e-5
MAGIC = 12582912.0

ALU = mybir.AluOpType
ACT = mybir.ActivationFunctionType
AX = mybir.AxisListType
F32 = mybir.dt.float32
F16 = mybir.dt.float16
I32 = mybir.dt.int32

C_BOFF, C_REF, C_BQ, C_BB, C_LOGA, C_DT, C_VLD, C_NEGP, C_N = 0, 2, 4, 8, 12, 16, 17, 18, 19

INPUTS = [
    ("x", (T, D), F32), ("ctx", (NB, P, B, KC, P), F32), ("mask", (P, B, 13), I32),
    ("wkv", (P, KC, 2 * D), F32), ("bkv", (1, 2 * D), F32), ("wq", (P, KC, D), F32),
    ("woff", (P, KC, 2, 104), F32), ("cols", (P, C_N), F32), ("loc", (1, T), F32),
    ("sel", (104, 40), F16), ("zsel", (P, 254), F32), ("bsel", (P, 64, P), F16),
    ("ident", (P, P), F32), ("vld", (NB, P, 1), F32), ("wo", (P, 8, D), F32),
    ("rows", (3, D), F32), ("wb", (P, KC, D), F32), ("wc", (P, KC, D), F32),
    ("wd", (P, KC, D), F32), ("rw", (P, KC, E), F32), ("rb", (1, E), F32),
    ("low", (1, 16 + 256), F32), ("wgu", (E, P, KC, 2 * I), F32), ("wdn", (E, P, 2, D), F32),
]


class Queue:

    def __init__(self, sem):
        self.sem, self.n, self.at, self.items, self.last = sem, 0, {}, [], None

    def do(self, fn, mark=None, wait=()):
        if mark:
            self.n += 1
            self.at[mark] = self.n
            self.last = mark
        self.items.append((fn, mark, wait))


def emit(q, eng, queues, dsem):
    seen = {}
    for fn, mark, wait in q.items:
        for w in wait:
            who, what = w.split(".", 1)
            sem, value = (dsem[what], 16) if who == "d" else (queues[who].sem, queues[who].at[what])
            if seen.get((who, what) if who == "d" else who, 0) < value:
                seen[(who, what) if who == "d" else who] = value
                eng.wait_ge(sem, value)
        ins = fn()
        if mark:
            ins.then_inc(q.sem, 1)


def program(nc, io, out):
    with ExitStack() as ctx:
        def sb(name, shape, dt=F32):
            return ctx.enter_context(nc.sbuf_tensor(name, shape, dt))

        def sem(name):
            return ctx.enter_context(nc.semaphore(name))

        acc_r = sb("acc_r", [P, 20480])
        kv_r = sb("kv_r", [P, 8192])
        wkv_r = sb("wkv_r", [P, 4096])
        ctx_r = sb("ctx_r", [P, 4096])
        qm_r = sb("qm_r", [P, 4096])
        w_r = sb("w_r", [P, 5120])
        ix = sb("ix", [104, 2 * T])
        rp = sb("rp", [104, 2 * T], F16)
        bkv = sb("bkv", [P, 2 * D])
        sel = sb("sel", [104, 40], F16)
        cols = sb("cols", [P, C_N])
        ident = sb("ident", [P, P])
        mk = sb("mk", [P, B, 13], I32)
        ones = sb("ones", [P, P])
        zsel = sb("zsel", [P, 254])
        st6 = sb("st6", [P, NT, 6])
        st2 = sb("st2", [P, NT, 2])
        rstd = sb("rstd", [P, NT])
        small = sb("small", [P, 64])
        flagi = sb("flagi", [1, 1], I32)
        vcol = sb("vcol", [P, 1])
        tmpg = sb("tmpg", [P, 320])
        rbt = sb("rbt", [P, E])
        lowt = sb("lowt", [P, 272])
        comb = sb("comb", [P, NT, E])
        psum = ctx.enter_context(nc.psum_tensor("psum", [P, 8, 512], F32))

        def bank(i):
            return psum[:, i, :]

        acc = acc_r[:, :].rearrange("p (u c) -> p u c", c=320)
        kv = kv_r[:, :].rearrange("p (b e) -> p b e", b=B)
        wkv = wkv_r[:, :].rearrange("p (k e) -> p k e", k=KC)
        ctxt = ctx_r[:, :].rearrange("p (b k m) -> p b k m", b=B, k=KC)
        qm = qm_r[:, :].rearrange("p (t n) -> p t n", t=8)
        hat = w_r[:, :].rearrange("p (s r n) -> p s r n", s=2, r=10)

        def part(base, off, n):
            return base[:, off:off + n]

        def tile4(base, off):
            return part(base, off, 2048).rearrange("p (k n) -> p k n", k=4)

        xa, xna, xta, wq, qpt = (tile4(acc_r, 2048 * i) for i in range(5))
        woff = part(acc_r, 10240, KC * 208).rearrange("p (k g c) -> p k g c", k=KC, g=2)
        pos = [acc_r[0:104, 11264 + 1024 * i:12288 + 1024 * i] for i in range(4)]
        loct = acc_r[0:104, 15360:15872]

        bsel = kv_r[:, 0:4096].bitcast(F16).rearrange("p (u c) -> p u c", c=P)
        wo = kv_r[:, 4096:8192].rearrange("p (t n) -> p t n", t=8)
        sc = w_r[:, 0:320]
        ex = w_r[:, 320:640]
        mn = w_r[:, 640:704]
        sm = w_r[:, 704:768]
        rc = w_r[:, 768:832]
        at_hi = w_r[:, 1024:1184].bitcast(F16)
        at_lo = w_r[:, 1184:1344].bitcast(F16)
        ctxp = wkv_r[:, :].rearrange("p (t n) -> p t n", t=8)
        xr = tile4(ctx_r, 0)
        rowt = ctx_r[:, 2048:2048 + 3 * D].rearrange("p (r n) -> p r n", r=3)
        wb, wc = tile4(qm_r, 0), tile4(qm_r, 2048)
        wd = tile4(w_r, 2048)
        xn2, xt2, bu, coef, xs, xn3, xt3 = (tile4(acc_r, 2048 * i) for i in range(7))
        abar = small[:, 0:4]
        dtc = small[:, 4:5]
        rw = w_r[:, 0:KC * E].rearrange("p (k e) -> p k e", k=KC)
        silu = acc_r[:, 0:1024]
        hid = acc_r[:, 1024:2048].rearrange("p (i n) -> p i n", i=2)
        NW = 4
        wbufs = [kv_r[:, 0:3072], kv_r[:, 3072:6144], acc_r[:, 14336:17408], acc_r[:, 17408:20480]]
        rt = [acc_r[:, 4096 + 1024 * i:5120 + 1024 * i] for i in range(4)]

        Q = {k: Queue(sem("s_" + k)) for k in "vaps"}
        V, A, PE, SP = Q["v"], Q["a"], Q["p"], Q["s"]
        dsem = {}
        ve, ae, pe, sp = nc.vector, nc.scalar, nc.tensor, nc.sync
        s_out = sem("s_out")

        def load(name, dst, src, wait=()):
            dsem[name] = sem("d_" + name)
            SP.do(lambda: sp.dma_start(dst, src).then_inc(dsem[name], 16), wait=wait)

        auto = [0]

        def v(fn, mark=None, wait=()):
            if mark is None:
                auto[0] += 1
                mark = f"auto{auto[0]}"
            own = ("v." + V.last,) if V.last else ()
            V.do(fn, mark, own + tuple(wait))

        def vi(fn, mark, wait=()):
            V.do(fn, mark, wait)

        load("x", xa, io["x"].rearrange("(m p) d -> p m d", p=P))
        load("cols", cols[:, :], io["cols"])
        load("ident", ident[:, :], io["ident"])
        load("wq", wq, io["wq"])
        load("woff", woff, io["woff"])
        load("mask", mk[:, :, :], io["mask"])
        load("loc", loct, io["loc"].broadcast_to([104, T]))
        load("ctx0", ctxt, io["ctx"][0])
        load("wkv", wkv, io["wkv"])
        load("bkv", bkv[:, :], io["bkv"].broadcast_to([P, 2 * D]))
        load("sel", sel[:, :], io["sel"])
        load("zsel", zsel[:, :], io["zsel"])
        load("rb", rbt[:, :], io["rb"].broadcast_to([P, E]))
        load("low", lowt[:, :], io["low"].broadcast_to([P, 272]))

        def layernorm(tag, src, dst, wait):
            for m in range(NT):
                vi(lambda m=m: ve.bn_stats(st6[:, m, :], src[:, m, :]), f"{tag}.st{m}", wait)
            for m in range(NT):
                vi(lambda m=m: ve.bn_aggr(st2[:, m, :], st6[:, m, :]), f"{tag}.ag{m}", (f"v.{tag}.st{m}",))
            v(lambda: ve.tensor_scalar(rstd[:, :], st2[:, :, 1], EPS, None, ALU.add), f"{tag}.var")
            A.do(lambda: ae.activation(rstd[:, :], rstd[:, :], ACT.Sqrt), f"{tag}.sd", (f"v.{tag}.var",))
            v(lambda: ve.reciprocal(rstd[:, :], rstd[:, :]), f"{tag}.rs", (f"a.{tag}.sd",))
            for m in range(NT):
                vi(lambda m=m: ve.tensor_scalar(dst[:, m, :], src[:, m, :], st2[:, m, 0:1], rstd[:, m:m + 1],
                                                ALU.subtract, ALU.mult), f"{tag}.xn{m}", (f"v.{tag}.rs",))

        def transposed(tag, src, dst, base, wait):
            for k in range(KC):
                for m in range(NT):
                    PE.do(lambda k=k, m=m: pe.transpose(psum[:, base + k, m * P:(m + 1) * P],
                                                        src[:, m, k * P:(k + 1) * P], ident[:, :]),
                          f"{tag}.t{k}" if m == NT - 1 else None,
                          (f"v.{tag}.xn{m}", "d.ident") + tuple(wait))
            for k in range(KC):
                A.do(lambda k=k: ae.activation(dst[:, k, :], bank(base + k), ACT.Copy), f"{tag}.xt{k}",
                     (f"p.{tag}.t{k}",))

        def product(banks, lhs, rhs, n, mark, wait=(), rows=P, cols_=D):
            for k in range(n):
                PE.do(lambda k=k: pe.matmul(banks[0:rows, 0:cols_], lhs(k), rhs(k), start=(k == 0), stop=(k == n - 1)),
                      mark if k == n - 1 else None, wait if k == 0 else ())

        vi(lambda: ve.memset(ones[:, :], 1.0), "ones")
        layernorm("l1", xa, xna, ("d.x",))
        transposed("l1", xna, xta, 0, ())
        vi(lambda: ve.memset(qm_r[:, :], 1.0), "qm1")

        for m in range(4):
            product(bank(4 + m), lambda k, m=m: wq[:, k, m * P:(m + 1) * P], lambda k: xta[:, k, :], KC, f"q{m}",
                    ("d.wq", "a.l1.xt3"))
            vi(lambda m=m: ve.tensor_scalar(qpt[:, m, :], bank(4 + m), cols[:, C_BQ + m:C_BQ + m + 1], None, ALU.add),
               f"q{m}", (f"p.q{m}", "d.cols"))
        for h in range(H):
            m, i = h // 4, h % 4
            lo = 64 * (h % 2)
            A.do(lambda m=m, i=i, lo=lo, h=h: ae.activation(qm[lo:lo + 32, h // 2, :], qpt[32 * i:32 * i + 32, m, :],
                                                            ACT.Copy),
                 f"qm{h}", (f"v.q{m}", "v.qm1"))

        for g in range(2):
            product(bank(g), lambda k, g=g: woff[:, k, g, :], lambda k: qpt[:, k, :], KC, f"off{g}",
                    ("d.woff", "v.q3"), rows=104)
        vi(lambda: ve.tensor_reduce(small[:, 8:16], mk[:, :, :], AX.X, ALU.add), "msum", ("d.mask",))
        PE.do(lambda: pe.matmul(psum[:, 2, 0:B], ones[:, :], small[:, 8:16], start=True, stop=True), "msum",
              ("v.msum", "v.ones", "a.l1.xt2"))

        def kv_proj(j):
            b, half = j // 2, j % 2
            product(bank(4 + j % 4), lambda k: ctxt[:, b, k, :], lambda k: wkv[:, k, half * D:(half + 1) * D], KC,
                    f"kv{j}", ("d.ctx0", "d.wkv", f"v.q{j}" if j < 4 else f"v.kv{j - 4}"))

        def kv_evac(j):
            b, half = j // 2, j % 2
            vi(lambda: ve.scalar_tensor_tensor(out=kv[:, b, half * D:(half + 1) * D],
                                               in0=bkv[:, half * D:(half + 1) * D], scalar=cols[:, C_VLD:C_VLD + 1],
                                               in1=bank(4 + j % 4), op0=ALU.mult, op1=ALU.add),
               f"kv{j}", (f"p.kv{j}", "d.bkv", "d.cols"))

        for j in range(16):
            kv_proj(j)

        t0, t1, t2, lf = pos
        c104 = cols[0:104, :]
        steps = []

        def pstep(fn, mark=None, wait=()):
            steps.append((fn, mark, wait))

        msb = small[0:104, 16:24]
        inv = small[0:104, 24:32]

        def by_batch(ap):
            return ap.unsqueeze(1).unsqueeze(3).broadcast_to([104, 2, B, S])

        def four(ap):
            return ap.rearrange("p (g b q) -> p g b q", g=2, b=B)

        pstep(lambda: ve.tensor_scalar(msb, psum[0:104, 2, 0:B], -1.0, float(M - 1), ALU.mult, ALU.add), "len",
              ("p.msum",))
        pstep(lambda: ve.reciprocal(inv, msb))
        pstep(lambda: ve.tensor_copy(four(lf), by_batch(msb)))
        for g in range(2):
            pstep(lambda g=g: ve.tensor_scalar(t0[:, g * T:(g + 1) * T], psum[0:104, g, :],
                                               c104[:, C_BOFF + g:C_BOFF + g + 1], c104[:, C_REF + g:C_REF + g + 1],
                                               ALU.add, ALU.add), f"off{g}", (f"p.off{g}",))
        pstep(lambda: ve.tensor_tensor(t0.rearrange("p (g n) -> p g n", g=2), t0.rearrange("p (g n) -> p g n", g=2),
                                       loct.unsqueeze(1).broadcast_to([104, 2, T]), ALU.add), "loc", ("d.loc",))
        pstep(lambda: ve.tensor_tensor(four(t1), four(t0), by_batch(inv), ALU.mult))
        pstep(lambda: ve.tensor_scalar(t1, t1, MAGIC, MAGIC, ALU.add, ALU.subtract))
        pstep(lambda: ve.tensor_tensor(t1, t1, lf, ALU.mult))
        pstep(lambda: ve.tensor_tensor(t0, t0, t1, ALU.subtract))
        pstep(lambda: ve.tensor_tensor(t1, t0, lf, ALU.mult))
        pstep(lambda: ve.scalar_tensor_tensor(out=t1, in0=t1, scalar=0.0, in1=lf, op0=ALU.is_lt, op1=ALU.mult))
        pstep(lambda: ve.tensor_tensor(t0, t0, t1, ALU.add))
        pstep(lambda: ve.tensor_scalar(t0, t0, 1.0 / (M - 1), 2.0, ALU.mult, ALU.mult))
        pstep(lambda: ve.tensor_scalar(t0, t0, -1.0, 1.0, ALU.add, ALU.add))
        pstep(lambda: ve.tensor_scalar(t0, t0, float(M), -1.0, ALU.mult, ALU.add))
        pstep(lambda: ve.tensor_scalar(ix[:, :], t0, 0.5, None, ALU.mult))
        pstep(lambda: ve.tensor_scalar(t1, ix[:, :], 800.0, float(M + 1), ALU.is_ge, ALU.mult))
        pstep(lambda: ve.tensor_tensor(t0, ix[:, :], t1, ALU.subtract))
        pstep(lambda: ve.tensor_scalar(t0, t0, float(DEAD + 1 - 64), None, ALU.add))
        pstep(lambda: ve.tensor_scalar(t1, t0, 0.5, None, ALU.add))
        pstep(lambda: ve.tensor_reduce(small[0:104, 32:33], t1, AX.X, ALU.max, apply_absolute_value=True), "far")
        pstep(lambda: ve.tensor_scalar(t1, t0, 66.0, -66.0, ALU.min, ALU.max))
        pstep(lambda: ve.tensor_copy(rp[:, :], t1))
        pstep(lambda: ve.tensor_tensor(rp[64:104, :], t1[64:104, :], rp[64:104, :], ALU.subtract), "rp")
        evacs = list(range(16))
        pos_at = 0
        while steps or evacs:
            for _ in range(3):
                if steps:
                    fn, mark, wait = steps.pop(0)
                    v(fn, mark and "pos." + mark, tuple(wait) + ("d.cols",))
            if evacs and pos_at >= 1 or not steps:
                kv_evac(evacs.pop(0)) if evacs else None
            pos_at += 1

        PE.do(lambda: pe.transpose(psum[0:1, 3, 0:104], small[0:104, 32:33], ident[0:104, 0:104]), "far",
              ("v.pos.far",))
        v(lambda: ve.tensor_reduce(small[0:1, 33:34], psum[0:1, 3, 0:104], AX.X, ALU.max), None, ("p.far",))
        v(lambda: ve.tensor_scalar(flagi[0:1, :], small[0:1, 33:34], 63.5, None, ALU.is_gt), "flag")

        units = [(t, half) for t in range(8) for half in range(2)]
        chunks = [(0, 4), (4, 8), (8, 10)]

        def head_row(t, r):
            h = 2 * t + r // 5
            return h // 8, (h % 8) * 5 + r % 5

        def spread(t, half, c, slot):
            out_ = []
            for i, r in enumerate(range(*chunks[c])):
                g, row = head_row(t, r)
                out_.append(lambda i=i, g=g, row=row: pe.matmul(
                    psum[:, 2 * slot + i // 2, (i % 2) * 256:(i % 2) * 256 + 256],
                    sel[:, row:row + 1].broadcast_to([104, P]),
                    rp[:, g * T + half * 256:g * T + half * 256 + 256], start=True, stop=True))
            return out_

        def hat_abs(s, c, slot):
            r0, r1 = chunks[c]
            n = (r1 - r0) * 256
            src = psum[:, 2 * slot:2 * slot + 2, :].rearrange("p a n -> p (a n)")[:, 0:n]
            return ae.activation(hat[:, s, r0:r1, :].rearrange("p r n -> p (r n)"), src, ACT.Abs,
                                 bias=cols[:, C_NEGP:C_NEGP + 1])

        def hat_low(s, c):
            w = hat[:, s, chunks[c][0]:chunks[c][1], :]
            return ve.tensor_scalar(w, w, 1.0, 1.0, ALU.min, ALU.subtract)

        def sampled(t, half, bb, s, g):
            b = 4 * half + bb
            out_ = []
            for i in range(2):
                h = 2 * t + i
                out_.append(lambda i=i, h=h: pe.matmul(
                    psum[64 * i:64 * i + 64, g, 0:320], kv[:, b, h * 64:(h + 1) * 64],
                    hat[:, s, 5 * i:5 * i + 5, bb * S:(bb + 1) * S], start=True, stop=True))
            return out_

        def weighed(out_, t, b, g):
            return ve.tensor_tensor(out_.rearrange("p (k q) -> p k q", k=NK),
                                    psum[:, g, 0:320].rearrange("p (k q) -> p k q", k=NK),
                                    qm[:, t, b * S:(b + 1) * S].unsqueeze(1).broadcast_to([P, NK, S]), ALU.mult)

        def pe_spread(n, c):
            t, half = units[n]
            x = 3 * n + c
            fns = spread(t, half, c, x % 2)
            w = ("v.pos.rp", "d.sel", "v.flag") + ((f"a.hat{x - 2}",) if x >= 2 else ("a.l1.xt3",))
            for i, fn in enumerate(fns):
                PE.do(fn, f"sp{x}" if i == len(fns) - 1 else None, w)

        def pe_sample(n):
            t, half = units[n]
            for bb in range(4):
                y = 4 * n + bb
                w = (f"v.low{3 * n + 2}", "v.kv15") + ((f"v.g{y - 4}",) if y >= 4 else ())
                fns = sampled(t, half, bb, n % 2, 4 + y % 4)
                for i, fn in enumerate(fns):
                    PE.do(fn, f"g{y}" if i == 1 else None, w)

        NU = len(units)
        for n in range(NU + 1):
            if n < NU:
                for c in range(3):
                    pe_spread(n, c)
                    x = 3 * n + c
                    A.do(lambda n=n, c=c, x=x: hat_abs(n % 2, c, x % 2), f"hat{x}",
                         (f"p.sp{x}",) + ((f"p.g{4 * (n - 2) + 3}",) if n >= 2 else ("v.flag",)))
                    vi(lambda n=n, c=c: hat_low(n % 2, c), f"low{x}", (f"a.hat{x}",))
            if n >= 1:
                pe_sample(n - 1)
                t, half = units[n - 1]
                for bb in range(4):
                    y = 4 * (n - 1) + bb
                    b = 4 * half + bb
                    vi(lambda t=t, b=b, y=y: weighed(acc[:, t * 8 + b, :], t, b, 4 + y % 4), f"g{y}",
                       (f"p.g{y}", "a.qm15"))

        g_d, g_kvp, g_kvv, g_rp, g_sp, g_hat, g_low, g_gp, g_gv, g_arr = (
            sem("g_" + n) for n in ("d", "kvp", "kvv", "rp", "sp", "hat", "low", "gp", "gv", "arr"))
        g_go = {e: sem("g_go" + e) for e in "vap"}
        g_all = [g_d, g_kvp, g_kvv, g_rp, g_sp, g_hat, g_low, g_gp, g_gv, g_arr]
        g_ini = sem("g_ini")

        def rest(eng, who, body, first=None, last=None):
            def run():
                val = eng.value_load(flagi[0:1, 0:1], min_val=0, max_val=1)
                with eng.If(val):
                    if first:
                        first()
                    with eng.Fori(1, NB) as j:
                        body(j)
                        if who != "s":
                            eng.sem_inc(g_arr, 1)
                            eng.wait_ge(g_go[who], 1)
                            eng.sem_clear(g_go[who])
                        else:
                            eng.wait_ge(g_arr, 3)
                            for s in g_all:
                                eng.sem_clear(s)
                            for s in g_go.values():
                                eng.sem_inc(s, 1)
            return run

        def rest_sp(j):
            sp.dma_start(ctx_r[:, :], io["ctx"].rearrange("j p b k m -> j p (b k m)")[bass.DynSlice(j, 1), :, :]
                         .rearrange("a p n -> (a p) n")).then_inc(g_d, 16)
            sp.dma_start(vcol[:, :], io["vld"][bass.DynSlice(j, 1), :, :].rearrange("a p n -> (a p) n")).then_inc(g_d, 16)
            sp.wait_ge(g_d, 32)

        def rest_v(j):
            ve.tensor_scalar(t1g, ix[:, :], 66.0, -66.0, ALU.min, ALU.max).then_inc(g_rp, 1)
            ve.wait_ge(g_rp, 1)
            ve.tensor_copy(rp[:, :], t1g).then_inc(g_rp, 1)
            ve.wait_ge(g_rp, 2)
            ve.tensor_tensor(rp[64:104, :], t1g[64:104, :], rp[64:104, :], ALU.subtract).then_inc(g_rp, 1)
            ve.wait_ge(g_rp, 3)
            ve.tensor_scalar(ix[:, :], ix[:, :], -128.0, None, ALU.add).then_inc(g_rp, 1)
            ve.wait_ge(g_rp, 4)
            ve.wait_ge(g_d, 32)
            for j2 in range(16):
                b, half = j2 // 2, j2 % 2
                ve.wait_ge(g_kvp, j2 + 1)
                ve.scalar_tensor_tensor(out=kv[:, b, half * D:(half + 1) * D], in0=bkv[:, half * D:(half + 1) * D],
                                        scalar=vcol[:, 0:1], in1=bank(4 + j2 % 4), op0=ALU.mult,
                                        op1=ALU.add).then_inc(g_kvv, 1)
            for n in range(NU):
                t, half = units[n]
                for c in range(3):
                    ve.wait_ge(g_hat, 3 * n + c + 1)
                    hat_low(0, c).then_inc(g_low, 1)
                for bb in range(4):
                    y = 4 * n + bb
                    b = 4 * half + bb
                    ve.wait_ge(g_gp, y + 1)
                    weighed(tmpg[:, :], t, b, 4 + y % 4).then_inc(g_gv, 1)
                    ve.wait_ge(g_gv, 2 * y + 1)
                    ve.tensor_tensor(acc[:, t * 8 + b, :], acc[:, t * 8 + b, :], tmpg[:, :], ALU.add).then_inc(g_gv, 1)
                    ve.wait_ge(g_gv, 2 * y + 2)

        t1g = w_r[0:104, 2560:3584]

        def rest_v_first():
            ve.tensor_scalar(ix[:, :], ix[:, :], float(DEAD + 1 - P - 64), None, ALU.add).then_inc(g_ini, 1)
            ve.wait_ge(g_ini, 1)

        def rest_a(j):
            for n in range(NU):
                for c in range(3):
                    x = 3 * n + c
                    ae.wait_ge(g_sp, x + 1)
                    if n >= 1:
                        ae.wait_ge(g_gp, 4 * n)
                    hat_abs(0, c, x % 2).then_inc(g_hat, 1)

        def rest_p(j):
            pe.wait_ge(g_d, 32)
            for j2 in range(16):
                b, half = j2 // 2, j2 % 2
                if j2 >= 4:
                    pe.wait_ge(g_kvv, j2 - 3)
                for k in range(KC):
                    mm = pe.matmul(bank(4 + j2 % 4), ctxt[:, b, k, :], wkv[:, k, half * D:(half + 1) * D],
                                   start=(k == 0), stop=(k == KC - 1))
                mm.then_inc(g_kvp, 1)
            pe.wait_ge(g_rp, 3)
            pe.wait_ge(g_kvv, 16)
            for n in range(NU):
                t, half = units[n]
                for c in range(3):
                    x = 3 * n + c
                    if x >= 2:
                        pe.wait_ge(g_hat, x - 1)
                    for fn in spread(t, half, c, x % 2):
                        mm = fn()
                    mm.then_inc(g_sp, 1)
                pe.wait_ge(g_low, 3 * n + 3)
                for bb in range(4):
                    y = 4 * n + bb
                    if y >= 4:
                        pe.wait_ge(g_gv, 2 * (y - 3))
                    for fn in sampled(t, half, bb, 0, 4 + y % 4):
                        mm = fn()
                    mm.then_inc(g_gp, 1)

        first_done = ("v.g63", "p.g63", "v.flag")
        SP.do(rest(sp, "s", rest_sp), wait=first_done)
        V.do(rest(ve, "v", rest_v, first=rest_v_first), wait=first_done)
        A.do(rest(ae, "a", rest_a), wait=first_done)
        PE.do(rest(pe, "p", rest_p), wait=first_done)
        vi(lambda: ve.memset(small[0:1, 40:41], 0.0), "rest")

        free = ("v.rest",)
        load("bsel", bsel, io["bsel"], free)
        load("wo", wo, io["wo"], free)
        load("x2", xr, io["x"].rearrange("(m p) d -> p m d", p=P), free)
        load("rows", rowt, io["rows"].unsqueeze(0).broadcast_to([P, 3, D]), free)
        load("wb", wb, io["wb"], free)
        load("wc", wc, io["wc"], free)
        load("wd", wd, io["wd"], free)

        for u in range(64):
            PE.do(lambda u=u: pe.matmul(psum[:, 0, 0:320], zsel[:, 126 - 2 * u:254 - 2 * u], acc[:, u, :],
                                        start=(u == 0), stop=(u == 63)), "score" if u == 63 else None,
                  ("v.rest", "d.zsel", "a.hat47"))

        def kq(ap):
            return ap.rearrange("p (k q) -> p k q", k=NK)

        def qk(ap):
            return ap.rearrange("p (k q) -> p q k", k=NK)

        def over_k(ap):
            return ap.unsqueeze(1).broadcast_to([P, NK, S])

        v(lambda: ve.tensor_copy(sc, psum[:, 0, 0:320]), None, ("p.score",))
        v(lambda: ve.tensor_reduce(mn, qk(sc), AX.X, ALU.min))
        v(lambda: ve.tensor_tensor(kq(sc), kq(sc), over_k(mn), ALU.subtract), "sc")
        A.do(lambda: ae.activation(ex, sc, ACT.Exp, scale=-0.5 / HD ** 0.5), "ex", ("v.sc",))
        v(lambda: ve.tensor_reduce(sm, qk(ex), AX.X, ALU.add), None, ("a.ex",))
        v(lambda: ve.reciprocal(rc, sm))
        v(lambda: ve.tensor_scalar(rc, rc, -0.5, None, ALU.mult))
        v(lambda: ve.tensor_tensor(kq(ex), kq(ex), over_k(rc), ALU.mult))
        v(lambda: ve.tensor_copy(at_hi, ex), "ahi")
        v(lambda: ve.tensor_tensor(at_lo, ex, at_hi, ALU.subtract), "at")

        for u in range(64):
            for i, a in enumerate((at_hi, at_lo)):
                PE.do(lambda u=u, i=i, a=a: pe.matmul(psum[:, 4 + u % 4, 0:320], bsel[:, u, :], a, start=(i == 0),
                                                      stop=(i == 1)), f"av{u}" if i else None,
                      ("v.at", "d.bsel") + ((f"v.av{u - 4}",) if u >= 4 else ()))
            vi(lambda u=u: ve.tensor_tensor(acc[:, u, :], acc[:, u, :], psum[:, 4 + u % 4, 0:320], ALU.mult),
               f"av{u}", (f"p.av{u}",))
            if u % 4 == 3:
                v(lambda u=u: ve.tensor_reduce(
                    wkv_r[:, (u - 3) * S:(u + 1) * S].rearrange("p (u q) -> p u q", u=4),
                    acc[:, u - 3:u + 1, :].rearrange("p u (k q) -> p u q k", k=NK), AX.X, ALU.add), f"ctx{u}")

        def add_row(r, dst, wait):
            vi(lambda: ve.tensor_tensor(dst, dst, rowt[:, r, :].unsqueeze(1).broadcast_to([P, NT, D]), ALU.add),
               f"row{r}", wait)

        add_row(0, xr, ("d.x2", "d.rows"))
        for m in range(NT):
            product(bank(m), lambda k, m=m: ctxp[:, k, m * P:(m + 1) * P], lambda k: wo[:, k, :], 8, f"o{m}",
                    ("v.ctx63", "d.wo", "v.sc"))
            v(lambda m=m: ve.tensor_tensor(xr[:, m, :], xr[:, m, :], bank(m), ALU.add), f"x1.{m}", (f"p.o{m}",))

        layernorm("l2", xr, xn2, ("v.x1.3",))
        transposed("l2", xn2, xt2, 4, ("v.av63",))
        v(lambda: None or ve.memset(small[:, 48:49], 0.0))
        A.do(lambda: ae.activation(dtc, cols[:, C_DT:C_DT + 1], ACT.Exp), "dt", ("d.cols",))
        A.do(lambda: ae.activation(abar, cols[:, C_LOGA:C_LOGA + 4], ACT.Exp), "ea", ("v.rest",))
        v(lambda: ve.tensor_scalar(abar, abar, dtc, -1.0, ALU.mult, ALU.mult), "adt", ("a.dt", "a.ea"))
        A.do(lambda: ae.activation(abar, abar, ACT.Exp), "abar", ("v.adt",))
        for k in range(KC):
            v(lambda k=k: ve.tensor_copy(coef[:, k, :], abar[:, k:k + 1].broadcast_to([P, T])), None, ("a.abar",))
        v(lambda: ve.memset(coef.rearrange("p k (b t) -> p k b t", b=B)[:, :, :, 0:1], 0.0), "coef")
        for m in range(4):
            product(bank(m), lambda k, m=m: wb[:, k, m * P:(m + 1) * P], lambda k: xt2[:, k, :], KC, f"bu{m}",
                    ("a.l2.xt3", "d.wb", "v.x1.3"))
            v(lambda m=m: ve.tensor_scalar(bu[:, m, :], bank(m), cols[:, C_BB + m:C_BB + m + 1], dtc, ALU.add,
                                           ALU.mult), f"bu{m}", (f"p.bu{m}",))
            v(lambda m=m: ve.tensor_tensor_scan(xs[:, m, :], coef[:, m, :], bu[:, m, :], 0.0, ALU.mult, ALU.add),
              f"xs{m}")
        add_row(1, xr, ("v.l2.xn3",))
        v(lambda: ve.tensor_copy(small[:, 49:50], small[:, 48:49]))
        add_row(2, xr, ("v.row1",))
        for m in range(NT):
            for i in range(2 * KC):
                lhs, w, k = (xt2, wd, i) if i < KC else (xs, wc, i - KC)
                PE.do(lambda m=m, i=i, lhs=lhs, w=w, k=k: pe.matmul(
                    bank(4 + m), lhs[:, k, m * P:(m + 1) * P], w[:, k, :], start=(i == 0), stop=(i == 7)),
                    f"y{m}" if i == 7 else None, ("d.wd", "d.wc") if i < KC else (f"v.xs{k}",))
            v(lambda m=m: ve.tensor_tensor(xr[:, m, :], xr[:, m, :], bank(4 + m), ALU.add), f"x2.{m}", (f"p.y{m}",))

        load("rw", rw, io["rw"], ("v.at", "v.ctx63", "p.av63"))
        for e in range(E):
            w = wbufs[e % NW]
            wait = (f"p.gd{e - NW}",) if e >= NW else (("p.o3", "p.av63") if e < 2 else ("v.ctx63",))
            load(f"wgu{e}", w[:, 0:2048].rearrange("p (k n) -> p k n", k=KC), io["wgu"][e], wait)
            load(f"wdn{e}", w[:, 2048:3072].rearrange("p (i n) -> p i n", i=2), io["wdn"][e], wait)

        layernorm("l3", xr, xn3, ("v.x2.3",))
        transposed("l3", xn3, xt3, 0, ("v.bu3",))
        for m in range(NT):
            for k in range(KC):
                PE.do(lambda m=m, k=k: pe.matmul(psum[:, 4, m * E:(m + 1) * E], xt3[:, k, m * P:(m + 1) * P],
                                                 rw[:, k, :], start=(k == 0), stop=(k == 3)),
                      "route" if m == 3 and k == 3 else None, ("a.l3.xt3", "d.rw", "v.x2.3"))
        s0, s1, s2, s3 = rt
        scr = s0[:, 0:64]
        cho = s0[:, 64:128]
        prs = s0[:, 128:144 + 80]
        grp = s0[:, 256:272]
        gsel = s0[:, 272:288]
        mch = s0[:, 320:384]
        msel = s0[:, 384:448]
        wsum = s0[:, 448:452]
        A.do(lambda: ae.activation(scr, psum[:, 4, 0:64], ACT.Sigmoid), "scr", ("p.route", "v.xs3"))
        v(lambda: ve.tensor_tensor(cho.rearrange("p (m e) -> p m e", m=NT), scr.rearrange("p (m e) -> p m e", m=NT),
                                   rbt[:, :].unsqueeze(1).broadcast_to([P, NT, E]), ALU.add), None,
          ("a.scr", "d.rb", "p.y3"))
        c4 = cho.rearrange("p (g i) -> p g i", i=4)
        pr = s0[:, 128:224].rearrange("p (g j) -> p g j", j=6)
        v(lambda: ve.tensor_tensor(pr[:, :, 0:3], c4[:, :, 0:1].broadcast_to([P, 16, 3]), c4[:, :, 1:4], ALU.add))
        v(lambda: ve.tensor_tensor(pr[:, :, 3:5], c4[:, :, 1:2].broadcast_to([P, 16, 2]), c4[:, :, 2:4], ALU.add))
        v(lambda: ve.tensor_tensor(pr[:, :, 5:6], c4[:, :, 2:3], c4[:, :, 3:4], ALU.add))
        v(lambda: ve.tensor_reduce(grp, pr, AX.X, ALU.max))

        def ranked(val, n, rows, low, gt, ge, out_, keep):
            vv = val.rearrange("p (r i) -> p r i", i=n)
            other = vv.unsqueeze(2).broadcast_to([P, rows, n, n])
            mine = vv.unsqueeze(3).broadcast_to([P, rows, n, n])
            g4 = gt.rearrange("p (r i j) -> p r i j", r=rows, i=n)
            e4 = ge.rearrange("p (r i j) -> p r i j", r=rows, i=n)
            g3 = gt.rearrange("p (r c) -> p r c", r=rows)
            e3 = ge.rearrange("p (r c) -> p r c", r=rows)
            lw = low.unsqueeze(1).broadcast_to([P, rows, n * n])
            v(lambda: ve.tensor_tensor(g4, other, mine, ALU.is_gt))
            v(lambda: ve.tensor_tensor(e4, other, mine, ALU.is_equal))
            v(lambda: ve.tensor_tensor(e3, e3, lw, ALU.mult))
            v(lambda: ve.tensor_tensor(gt, gt, ge, ALU.add))
            v(lambda: ve.tensor_reduce(out_, g4, AX.X, ALU.add))
            v(lambda: ve.tensor_scalar(out_, out_, float(keep), None, ALU.is_lt))

        vi(lambda: ve.memset(small[:, 50:51], 0.0), "lowok", ("d.low",))
        ranked(grp, 4, NT, lowt[:, 0:16], s1[:, 0:64], s1[:, 64:128], gsel, 2)
        g3 = gsel.unsqueeze(2).broadcast_to([P, 16, 4])
        m3 = mch.rearrange("p (g i) -> p g i", i=4)
        v(lambda: ve.tensor_tensor(m3, c4, g3, ALU.mult))
        v(lambda: ve.tensor_scalar(gsel, gsel, 1.0, 1e9, ALU.subtract, ALU.mult))
        v(lambda: ve.tensor_tensor(m3, m3, g3, ALU.add))
        ranked(mch, E, NT, lowt[:, 16:272], s2, s3, msel, 4)
        v(lambda: ve.tensor_tensor(msel, msel, scr, ALU.mult))
        v(lambda: ve.tensor_reduce(wsum, msel.rearrange("p (m e) -> p m e", m=NT), AX.X, ALU.add))
        v(lambda: ve.tensor_scalar(wsum, wsum, 1e-20, None, ALU.add))
        v(lambda: ve.reciprocal(wsum, wsum))
        v(lambda: ve.tensor_scalar(wsum, wsum, 2.5, None, ALU.mult))
        v(lambda: ve.tensor_tensor(comb[:, :, :], msel.rearrange("p (m e) -> p m e", m=NT),
                                   wsum.unsqueeze(2).broadcast_to([P, NT, E]), ALU.mult), "comb")

        def weights(e):
            w = wbufs[e % NW]
            return w[:, 0:2048].rearrange("p (k n) -> p k n", k=KC), w[:, 2048:3072].rearrange("p (i n) -> p i n", i=2)

        def gate_up(e):
            gu, _ = weights(e)
            for i in range(4):
                product(bank(i), lambda k, i=i: gu[:, k, i * P:(i + 1) * P], lambda k: xt3[:, k, :], KC, f"gu{e}.{i}",
                        (f"d.wgu{e}",) + ((f"v.h{e - 1}",) if e else ("a.l3.xt3",)))

        def hidden(e):
            A.do(lambda: ae.activation(silu, psum[:, 0:2, :].rearrange("p a n -> p (a n)"), ACT.Silu), f"si{e}",
                 (f"p.gu{e}.1",) + ((f"v.h{e - 1}",) if e else ("p.l2.t3", "p.y3", "v.x2.3")))
            vi(lambda: ve.tensor_tensor(hid.rearrange("p i n -> p (i n)"), silu,
                                        psum[:, 2:4, :].rearrange("p a n -> p (a n)"), ALU.mult), f"h{e}",
               (f"a.si{e}", f"p.gu{e}.3") + ((f"p.gd{e - 1}",) if e else ("v.comb",)))

        def down(e):
            _, dn = weights(e)
            for m in range(NT):
                product(bank(4 + m), lambda k, m=m: hid[:, k, m * P:(m + 1) * P], lambda k: dn[:, k, :], 2,
                        f"gd{e}" if m == NT - 1 else f"gd{e}.{m}",
                        (f"d.wdn{e}", f"v.h{e}", f"v.e{e - 1}.{m}" if e else "a.scr"))

        def add_expert(e):
            for m in range(NT):
                vi(lambda m=m: ve.scalar_tensor_tensor(out=xr[:, m, :], in0=bank(4 + m), scalar=comb[:, m, e:e + 1],
                                                       in1=xr[:, m, :], op0=ALU.mult, op1=ALU.add), f"e{e}.{m}",
                   (f"p.gd{e}" if m == NT - 1 else f"p.gd{e}.{m}", f"v.e{e - 1}.{m}" if e else "v.comb"))

        gate_up(0)
        hidden(0)
        for e in range(E):
            down(e)
            if e + 1 < E:
                gate_up(e + 1)
            add_expert(e)
            if e + 1 < E:
                hidden(e + 1)
        for m in range(NT):
            SP.do(lambda m=m: sp.dma_start(out.rearrange("(m p) d -> p m d", p=P)[:, m, :], xr[:, m, :])
                  .then_inc(s_out, 16), wait=(f"v.e{E - 1}.{m}",))
        SP.do(lambda: sp.wait_ge(s_out, 16 * NT))

        block = ctx.enter_context(nc.Block())

        @block.sync
        def _(eng):
            emit(SP, eng, Q, dsem)

        @block.vector
        def _(eng):
            emit(V, eng, Q, dsem)

        @block.scalar
        def _(eng):
            emit(A, eng, Q, dsem)

        @block.tensor
        def _(eng):
            emit(PE, eng, Q, dsem)


def laid_out(a):
    def kt(w):
        return np.ascontiguousarray(w.T.reshape(KC, P, w.shape[0]).transpose(1, 0, 2))

    f = np.float32
    c = a["ctx_1024"]
    ring = np.zeros((B, NB * P, D), c.dtype)
    ring[:, 0:DEAD] = c[:, M - DEAD:]
    ring[:, DEAD + 1:M + 1] = c[:, :M - DEAD]
    ctx = ring.reshape(B, NB, P, KC, P).transpose(1, 4, 0, 3, 2)
    mask = np.zeros((B, P * 13), a["mask_BxS2_if0"].dtype)
    mask[:, :M] = a["mask_BxS2_if0"]
    wk, wv = a["L0_xattn_Wk"], a["L0_xattn_Wv"]
    wkv = np.stack([wk.reshape(H, HD, D), wv.reshape(H, HD, D)], 1).reshape(2 * D, D)
    bkv = np.stack([a["L0_xattn_bk"].reshape(H, HD), a["L0_xattn_bv"].reshape(H, HD)], 1).reshape(1, 2 * D)
    woff = np.zeros((2, 104, D), f)
    boff = np.zeros((2, 104), f)
    ref = np.zeros((2, 104), f)
    for g in range(2):
        for o in (0, 64):
            woff[g, o:o + 40] = a["L0_xattn_Woff"][40 * g:40 * g + 40]
            boff[g, o:o + 40] = a["L0_xattn_boff"][40 * g:40 * g + 40]
            ref[g, o:o + 40] = np.tile(np.arange(NK) - 3, 8)
    cols = np.zeros((P, C_N), f)
    cols[0:104, C_BOFF:C_BOFF + 2] = boff.T
    cols[0:104, C_REF:C_REF + 2] = ref.T
    cols[:, C_BQ:C_BQ + 4] = a["L0_xattn_bq"].reshape(4, P).T
    cols[:, C_BB:C_BB + 4] = a["L0_attn_b_B"].reshape(4, P).T
    cols[:, C_LOGA:C_LOGA + 4] = a["L0_attn_log_A"].reshape(4, P).T
    cols[:, C_DT] = a["L0_attn_log_dt"][0]
    p = np.arange(P)
    row = np.arange(NB * P).reshape(NB, P, 1)
    vld = ((row != DEAD) & (row <= M)).astype(f)
    cols[:, C_VLD] = vld[0, :, 0]
    cols[:, C_NEGP] = 64 - p
    sel = np.zeros((104, 40), np.float16)
    sel[np.arange(40), np.arange(40)] = 1
    sel[64 + np.arange(40), np.arange(40)] = 1
    zsel = np.zeros((P, 254), f)
    zsel[0:32, 126] = 1
    zsel[64:96, 127] = 1
    bsel = np.zeros((P, 64, P), np.float16)
    for u in range(64):
        bsel[2 * u, u, 32:64] = 1
        bsel[2 * u + 1, u, 96:128] = 1
    wo = np.zeros((P, 8, D), f)
    wot = a["L0_xattn_Wo"].T.reshape(8, 2, HD, D)
    wo[32:64] = wot[:, 0].transpose(1, 0, 2)
    wo[96:128] = wot[:, 1].transpose(1, 0, 2)
    low4 = (np.arange(4)[None, :] < np.arange(4)[:, None]).astype(f)
    low16 = (np.arange(16)[None, :] < np.arange(16)[:, None]).astype(f)
    wg, wu = a["L0_ffn_w_gate"], a["L0_ffn_w_up"]
    wgu = np.concatenate([wg, wu], 1).transpose(0, 2, 1).reshape(E, KC, P, 2 * I).transpose(0, 2, 1, 3)
    wdn = a["L0_ffn_w_down"].transpose(0, 2, 1).reshape(E, 2, P, D).transpose(0, 2, 1, 3)
    return {
        "x": a["x"].reshape(T, D), "ctx": ctx, "mask": mask.reshape(B, P, 13).transpose(1, 0, 2), "wkv": kt(wkv),
        "bkv": bkv, "wq": kt(a["L0_xattn_Wq"]),
        "woff": woff.transpose(2, 0, 1).reshape(KC, P, 2, 104).transpose(1, 0, 2, 3), "cols": cols,
        "loc": np.tile(np.arange(S), B).astype(f)[None], "sel": sel, "zsel": zsel, "bsel": bsel,
        "ident": np.eye(P, dtype=f), "vld": vld, "wo": wo,
        "rows": np.stack([a["L0_xattn_bo"], a["L0_attn_b_C"], a["L0_attn_b_D"]]), "wb": kt(a["L0_attn_W_B"]),
        "wc": kt(a["L0_attn_W_C"]), "wd": kt(a["L0_attn_W_D"]), "rw": kt(a["L0_ffn_router_weight"]),
        "rb": a["L0_ffn_router_bias"][None], "low": np.concatenate([low4.ravel(), low16.ravel()])[None],
        "wgu": wgu, "wdn": wdn,
    }


def kernel(**inputs):
    import concourse.bacc as _bacc
    from concourse import mybir as _mybir
    from concourse.bass_utils import run_bass_kernel_spmd as _run

    nc = _bacc.Bacc("TRN2", target_bir_lowering=False, num_devices=1)
    data = laid_out({k: np.asarray(v) for k, v in inputs.items()})
    arrays, io = {}, {}
    for name, shape, dt in INPUTS:
        a = np.ascontiguousarray(data[name])
        assert a.shape == shape, (name, a.shape)
        arrays[f"in_{name}"] = a
        io[name] = nc.dram_tensor(f"in_{name}", shape, dt, kind="ExternalInput").ap()
    out = nc.dram_tensor("out_0", (T, D), F32, kind="ExternalOutput").ap()
    program(nc, io, out)
    r = _run(nc, [arrays], core_ids=[0])
    return r.results[0]["out_0"].reshape(B, S, D)
```

```python
from contextlib import ExitStack

import numpy as np

import concourse.bass as bass
from concourse import mybir

P = 128
B, S, D, M = 8, 64, 512, 1601
T = B * S
NT = T // P
KC = D // P
H, NK = 16, 5
HD = D // H
NB = 13
DEAD = 32
E, I = 16, 256
EPS = 1e-5
MAGIC = 12582912.0

ALU = mybir.AluOpType
ACT = mybir.ActivationFunctionType
AX = mybir.AxisListType
F32 = mybir.dt.float32
F16 = mybir.dt.float16
I32 = mybir.dt.int32

C_BOFF, C_REF, C_BQ, C_BB, C_LOGA, C_DT, C_VLD, C_NEGP, C_N = 0, 2, 4, 8, 12, 16, 17, 18, 19

INPUTS = [
    ("x", (T, D), F32), ("ctx", (NB, P, B, KC, P), F32), ("mask", (P, B, 13), I32),
    ("wkv", (P, KC, 2 * D), F32), ("bkv", (1, 2 * D), F32), ("wq", (P, KC, D), F32),
    ("woff", (P, KC, 2, 104), F32), ("cols", (P, C_N), F32), ("loc", (1, T), F32),
    ("sel", (104, 40), F16), ("zsel", (P, 2, 126), F32), ("bsel", (P, 32, P), F16),
    ("ident", (P, P), F32), ("vld", (NB, P, 1), F32), ("wo", (P, 4, D), F32),
    ("rows", (3, D), F32), ("wb", (P, KC, D), F32), ("wc", (P, KC, D), F32),
    ("wd", (P, KC, D), F32), ("rw", (P, KC, E), F32), ("rb", (1, E), F32),
    ("low", (1, 16 + 256), F32), ("ltri", (P, P), F32), ("iota", (1, T), F16),
    ("tokc", (P, 5), F32), ("wgu", (E, P, KC, 2 * I), F32), ("wdn", (E, P, 2, D), F32),
]


class Queue:

    def __init__(self, sem):
        self.sem, self.n, self.at, self.items, self.last = sem, 0, {}, [], None

    def do(self, fn, mark=None, wait=()):
        if mark:
            self.n += 1
            self.at[mark] = self.n
            self.last = mark
        self.items.append((fn, mark, wait))


def emit(q, eng, queues, dsem):
    seen = {}
    for fn, mark, wait in q.items:
        for w in wait:
            who, what = w.split(".", 1)
            sem, value = (dsem[what], 16) if who == "d" else (queues[who].sem, queues[who].at[what])
            if seen.get((who, what) if who == "d" else who, 0) < value:
                seen[(who, what) if who == "d" else who] = value
                eng.wait_ge(sem, value)
        ins = fn()
        if mark:
            ins.then_inc(q.sem, 1)


def program(nc, io, out):
    with ExitStack() as ctx:
        def sb(name, shape, dt=F32):
            return ctx.enter_context(nc.sbuf_tensor(name, shape, dt))

        def sem(name):
            return ctx.enter_context(nc.semaphore(name))

        acc_r = sb("acc_r", [P, 20480])
        kv_r = sb("kv_r", [P, 8192])
        wkv_r = sb("wkv_r", [P, 4096])
        ctx_r = sb("ctx_r", [P, 4096])
        qm_r = sb("qm_r", [P, 4096])
        w_r = sb("w_r", [P, 5120])
        ix = sb("ix", [104, 2 * T])
        rp = sb("rp", [104, 2 * T], F16)
        bkv = sb("bkv", [P, 2 * D])
        sel = sb("sel", [104, 40], F16)
        cols = sb("cols", [P, C_N])
        ident = sb("ident", [P, P])
        mk = sb("mk", [P, B, 13], I32)
        ones = sb("ones", [P, P])
        zsel = sb("zsel", [P, 2, 126])
        st6 = sb("st6", [P, NT, 6])
        st2 = sb("st2", [P, NT, 2])
        rstd = sb("rstd", [P, NT])
        small = sb("small", [P, 64])
        flagi = sb("flagi", [1, 1], I32)
        vcol = sb("vcol", [P, 1])
        tmpg = sb("tmpg", [P, 320])
        rbt = sb("rbt", [P, E])
        lowt = sb("lowt", [P, 272])
        comb = sb("comb", [P, NT, E])
        tokc = sb("tokc", [P, 5])
        cnt = sb("cnt", [1, E], I32)
        slot_rows = sb("slot_rows", [P, (E - 1) * NT], I32)
        psum = ctx.enter_context(nc.psum_tensor("psum", [P, 8, 512], F32))

        def bank(i):
            return psum[:, i, :]

        acc = acc_r[:, :].rearrange("p (u c) -> p u c", c=320)
        kv = kv_r[:, :].rearrange("p (b e) -> p b e", b=B)
        wkv = wkv_r[:, :].rearrange("p (k e) -> p k e", k=KC)
        ctxt = ctx_r[:, :].rearrange("p (b k m) -> p b k m", b=B, k=KC)
        qm = qm_r[:, :].rearrange("p (t n) -> p t n", t=8)
        hat = w_r[:, :].rearrange("p (s r n) -> p s r n", s=2, r=10)

        def part(base, off, n):
            return base[:, off:off + n]

        def tile4(base, off):
            return part(base, off, 2048).rearrange("p (k n) -> p k n", k=4)

        xa, xna, xta, wq, qpt = (tile4(acc_r, 2048 * i) for i in range(5))
        woff = part(acc_r, 10240, KC * 208).rearrange("p (k g c) -> p k g c", k=KC, g=2)
        pos = [acc_r[0:104, 11264 + 1024 * i:12288 + 1024 * i] for i in range(4)]
        loct = acc_r[0:104, 15360:15872]

        bsel = kv_r[:, 0:2048].bitcast(F16).rearrange("p (u c) -> p u c", c=P)
        wo = kv_r[:, 2048:4096].rearrange("p (t n) -> p t n", t=4)
        ctxp = wkv_r[:, 0:2048].rearrange("p (t n) -> p t n", t=4)
        xr = tile4(ctx_r, 0)
        rowt = ctx_r[:, 2048:2048 + 3 * D].rearrange("p (r n) -> p r n", r=3)
        wb, wc = tile4(qm_r, 0), tile4(qm_r, 2048)
        wd = tile4(w_r, 2048)
        xn2, xt2, bu, coef, xs, xn3, xt3 = (tile4(acc_r, 2048 * i) for i in range(7))
        abar = small[:, 0:4]
        dtc = small[:, 4:5]
        rw = w_r[:, 0:KC * E].rearrange("p (k e) -> p k e", k=KC)
        xh = acc_r[:, 0:1024].bitcast(F16).rearrange("p (m d) -> p m d", m=NT)
        xl = acc_r[:, 1024:2048].bitcast(F16).rearrange("p (m d) -> p m d", m=NT)
        iota = acc_r[:, 2048:2304].bitcast(F16)
        picks = [acc_r[:, 2304 + 256 * i:2560 + 256 * i].bitcast(F16).rearrange("p (m s) -> p m s", m=NT)
                 for i in range(4)]
        xg = acc_r[:, 3328:3840]
        ltri = acc_r[:, 3840:3968]
        silu0 = acc_r[:, 8192:9216]
        hid0 = acc_r[:, 9216:10240].rearrange("p (i n) -> p i n", i=2)
        ys = [acc_r[:, 8192 + 512 * i:8704 + 512 * i] for i in range(10)]
        silu = w_r[:, 512:768]
        hid = w_r[:, 768:1024]
        hidt = w_r[:, 1024:1280]
        rh = w_r[:, 1280:1408].bitcast(F16).rearrange("p (m e c) -> p m e c", m=NT, e=E)
        posm = w_r[:, 1408:1472]
        selc = w_r[:, 1472:1552].rearrange("p (m e) -> p m e", m=5)
        lst = w_r[:, 1552:1556]
        pad = w_r[:, 1556:1557]
        wcol = w_r[:, 1557:1558]
        NW = 4
        wbufs = [kv_r[:, 0:3072], kv_r[:, 3072:6144], acc_r[:, 14336:17408], acc_r[:, 17408:20480]]
        rt = [acc_r[:, 4096 + 1024 * i:5120 + 1024 * i] for i in range(4)]

        Q = {k: Queue(sem("s_" + k)) for k in "vapsg"}
        V, A, PE, SP, GP = Q["v"], Q["a"], Q["p"], Q["s"], Q["g"]
        dsem = {}
        ve, ae, pe, sp, gp = nc.vector, nc.scalar, nc.tensor, nc.sync, nc.gpsimd
        s_out = sem("s_out")

        def load(name, dst, src, wait=()):
            dsem[name] = sem("d_" + name)
            SP.do(lambda: sp.dma_start(dst, src).then_inc(dsem[name], 16), wait=wait)

        auto = [0]

        def v(fn, mark=None, wait=()):
            if mark is None:
                auto[0] += 1
                mark = f"auto{auto[0]}"
            own = ("v." + V.last,) if V.last else ()
            V.do(fn, mark, own + tuple(wait))

        def vi(fn, mark, wait=()):
            V.do(fn, mark, wait)

        for m in range(NT):
            load(f"xin{m}", xa[:, m, :], io["x"].rearrange("(m p) d -> p m d", p=P)[:, m, :])
        load("cols", cols[:, :], io["cols"])
        load("ident", ident[:, :], io["ident"])
        load("wq", wq, io["wq"])
        load("woff", woff, io["woff"])
        load("mask", mk[:, :, :], io["mask"])
        load("sel", sel[:, :], io["sel"])
        load("loc", loct, io["loc"].broadcast_to([104, T]))
        load("ctx0", ctxt, io["ctx"][0])
        load("wkv", wkv, io["wkv"])
        load("bkv", bkv[:, :], io["bkv"].broadcast_to([P, 2 * D]))
        load("zsel", zsel[:, :, :], io["zsel"])
        load("rb", rbt[:, :], io["rb"].broadcast_to([P, E]))
        load("low", lowt[:, :], io["low"].broadcast_to([P, 272]))
        load("tokc", tokc[:, :], io["tokc"])

        def stats(tag, src, m, wait):
            vi(lambda: ve.bn_stats(st6[:, m, :], src[:, m, :]), f"{tag}.st{m}", wait)

        def normalise(tag, src, dst, m):
            r = rstd[:, m:m + 1]
            v(lambda: ve.bn_aggr(st2[:, m, :], st6[:, m, :]), f"{tag}.ag{m}", (f"v.{tag}.st{m}",))
            v(lambda: ve.tensor_scalar(r, st2[:, m, 1:2], EPS, None, ALU.add), f"{tag}.var{m}")
            A.do(lambda: ae.activation(r, r, ACT.Sqrt), f"{tag}.sd{m}", (f"v.{tag}.var{m}",))
            v(lambda: ve.reciprocal(r, r), f"{tag}.rs{m}", (f"a.{tag}.sd{m}",))
            v(lambda: ve.tensor_scalar(dst[:, m, :], src[:, m, :], st2[:, m, 0:1], r, ALU.subtract, ALU.mult),
              f"{tag}.xn{m}")

        def transposes(tag, src, base, m, wait=()):
            for k in range(KC):
                PE.do(lambda k=k: pe.transpose(psum[:, base + k, m * P:(m + 1) * P],
                                               src[:, m, k * P:(k + 1) * P], ident[:, :]),
                      f"{tag}.t{k}" if m == NT - 1 else None, (f"v.{tag}.xn{m}", "d.ident") + tuple(wait))

        def transposed(tag, dst, base):
            for k in range(KC):
                if k % 2:
                    A.do(lambda k=k: ae.activation(dst[:, k, :], bank(base + k), ACT.Copy), f"{tag}.xt{k}",
                         (f"p.{tag}.t{k}",))
                else:
                    vi(lambda k=k: ve.tensor_copy(dst[:, k, :], bank(base + k)), f"{tag}.xt{k}", (f"p.{tag}.t{k}",))

        def product(banks, lhs, rhs, n, mark, wait=(), rows=P, cols_=D):
            for k in range(n):
                PE.do(lambda k=k: pe.matmul(banks[0:rows, 0:cols_], lhs(k), rhs(k), start=(k == 0), stop=(k == n - 1)),
                      mark if k == n - 1 else None, wait if k == 0 else ())

        vi(lambda: ve.memset(ones[:, :], 1.0), "ones")
        for m in range(NT):
            stats("l1", xa, m, (f"d.xin{m}",))
            normalise("l1", xa, xna, m)
            transposes("l1", xna, 0, m)
        transposed("l1", xta, 0)
        vi(lambda: ve.memset(qm_r[:, :], 1.0), "qm1")

        for m in range(4):
            product(bank(4 + m), lambda k, m=m: wq[:, k, m * P:(m + 1) * P], lambda k: xta[:, k, :], KC, f"q{m}",
                    ("d.wq", "a.l1.xt3", "v.l1.xt2"))
            vi(lambda m=m: ve.tensor_scalar(qpt[:, m, :], bank(4 + m), cols[:, C_BQ + m:C_BQ + m + 1], None, ALU.add),
               f"q{m}", (f"p.q{m}", "d.cols"))
        for h in range(H):
            m, i = h // 4, h % 4
            lo = 64 * (h % 2) + 32 * (h // 2 % 2)
            A.do(lambda m=m, i=i, lo=lo, h=h: ae.activation(qm[lo:lo + 32, h // 2, :], qpt[32 * i:32 * i + 32, m, :],
                                                            ACT.Copy),
                 f"qm{h}", (f"v.q{m}", "v.qm1"))

        for g in range(2):
            product(bank(g), lambda k, g=g: woff[:, k, g, :], lambda k: qpt[:, k, :], KC, f"off{g}",
                    ("d.woff", "v.q3"), rows=104)
        vi(lambda: ve.tensor_reduce(small[:, 8:16], mk[:, :, :], AX.X, ALU.add), "msum", ("d.mask",))
        PE.do(lambda: pe.matmul(psum[:, 2, 0:B], ones[:, :], small[:, 8:16], start=True, stop=True), "msum",
              ("v.msum", "v.ones", "v.l1.xt2"))

        def kv_proj(j):
            b, half = j // 2, j % 2
            product(bank(4 + j % 4), lambda k: ctxt[:, b, k, :], lambda k: wkv[:, k, half * D:(half + 1) * D], KC,
                    f"kv{j}", ("d.ctx0", "d.wkv", f"v.q{j}" if j < 4 else f"v.kv{j - 4}"))

        def kv_evac(j):
            b, half = j // 2, j % 2
            vi(lambda: ve.scalar_tensor_tensor(out=kv[:, b, half * D:(half + 1) * D],
                                               in0=bkv[:, half * D:(half + 1) * D], scalar=cols[:, C_VLD:C_VLD + 1],
                                               in1=bank(4 + j % 4), op0=ALU.mult, op1=ALU.add),
               f"kv{j}", (f"p.kv{j}", "d.bkv", "d.cols"))

        for j in range(16):
            kv_proj(j)

        t0, t1, t2, lf = pos
        c104 = cols[0:104, :]
        steps = []

        def pstep(fn, mark=None, wait=()):
            steps.append((fn, mark, wait))

        msb = small[0:104, 16:24]
        inv = small[0:104, 24:32]

        def by_batch(ap):
            return ap.unsqueeze(1).unsqueeze(3).broadcast_to([104, 2, B, S])

        def four(ap):
            return ap.rearrange("p (g b q) -> p g b q", g=2, b=B)

        pstep(lambda: ve.tensor_scalar(msb, psum[0:104, 2, 0:B], -1.0, float(M - 1), ALU.mult, ALU.add), "len",
              ("p.msum",))
        pstep(lambda: ve.reciprocal(inv, msb))
        pstep(lambda: ve.tensor_copy(four(lf), by_batch(msb)))
        for g in range(2):
            pstep(lambda g=g: ve.tensor_scalar(t0[:, g * T:(g + 1) * T], psum[0:104, g, :],
                                               c104[:, C_BOFF + g:C_BOFF + g + 1], c104[:, C_REF + g:C_REF + g + 1],
                                               ALU.add, ALU.add), f"off{g}", (f"p.off{g}",))
        pstep(lambda: ve.tensor_tensor(t0.rearrange("p (g n) -> p g n", g=2), t0.rearrange("p (g n) -> p g n", g=2),
                                       loct.unsqueeze(1).broadcast_to([104, 2, T]), ALU.add), "loc", ("d.loc",))
        pstep(lambda: ve.tensor_tensor(four(t1), four(t0), by_batch(inv), ALU.mult))
        pstep(lambda: ve.tensor_scalar(t1, t1, MAGIC, MAGIC, ALU.add, ALU.subtract))
        pstep(lambda: ve.tensor_tensor(t1, t1, lf, ALU.mult))
        pstep(lambda: ve.tensor_tensor(t0, t0, t1, ALU.subtract))
        pstep(lambda: ve.tensor_tensor(t1, t0, lf, ALU.mult))
        pstep(lambda: ve.scalar_tensor_tensor(out=t1, in0=t1, scalar=0.0, in1=lf, op0=ALU.is_lt, op1=ALU.mult))
        pstep(lambda: ve.tensor_tensor(t0, t0, t1, ALU.add))
        pstep(lambda: ve.tensor_scalar(t0, t0, 1.0 / (M - 1), 2.0, ALU.mult, ALU.mult))
        pstep(lambda: ve.tensor_scalar(t0, t0, -1.0, 1.0, ALU.add, ALU.add))
        pstep(lambda: ve.tensor_scalar(t0, t0, float(M), -1.0, ALU.mult, ALU.add))
        pstep(lambda: ve.tensor_scalar(ix[:, :], t0, 0.5, None, ALU.mult))
        pstep(lambda: ve.tensor_scalar(t1, ix[:, :], 800.0, float(M + 1), ALU.is_ge, ALU.mult))
        pstep(lambda: ve.tensor_tensor(t0, ix[:, :], t1, ALU.subtract))
        pstep(lambda: ve.tensor_scalar(t0, t0, float(DEAD + 1 - 64), None, ALU.add))
        pstep(lambda: ve.tensor_scalar(t1, t0, 0.5, None, ALU.add))
        pstep(lambda: ve.tensor_reduce(small[0:104, 32:33], t1, AX.X, ALU.max, apply_absolute_value=True), "far")
        pstep(lambda: ve.tensor_scalar(t1, t0, 66.0, -66.0, ALU.min, ALU.max))
        pstep(lambda: ve.tensor_copy(rp[:, :], t1))
        pstep(lambda: ve.tensor_tensor(rp[64:104, :], t1[64:104, :], rp[64:104, :], ALU.subtract), "rp")
        evacs = list(range(16))
        pos_at = 0
        while steps or evacs:
            for _ in range(3):
                if steps:
                    fn, mark, wait = steps.pop(0)
                    v(fn, mark and "pos." + mark, tuple(wait) + ("d.cols",))
            if evacs and pos_at >= 1 or not steps:
                kv_evac(evacs.pop(0)) if evacs else None
            pos_at += 1

        PE.do(lambda: pe.transpose(psum[0:1, 3, 0:104], small[0:104, 32:33], ident[0:104, 0:104]), "far",
              ("v.pos.far",))
        v(lambda: ve.tensor_reduce(small[0:1, 33:34], psum[0:1, 3, 0:104], AX.X, ALU.max), None, ("p.far",))
        v(lambda: ve.tensor_scalar(flagi[0:1, :], small[0:1, 33:34], 63.5, None, ALU.is_gt), "flag")

        units = [(t, half) for t in range(8) for half in range(2)]
        chunks = [(0, 4), (4, 8), (8, 10)]

        def head_row(t, r):
            h = 2 * t + r // 5
            return h // 8, (h % 8) * 5 + r % 5

        def spread(t, half, c, slot):
            out_ = []
            for i, r in enumerate(range(*chunks[c])):
                g, row = head_row(t, r)
                out_.append(lambda i=i, g=g, row=row: pe.matmul(
                    psum[:, 2 * slot + i // 2, (i % 2) * 256:(i % 2) * 256 + 256],
                    sel[:, row:row + 1].broadcast_to([104, P]),
                    rp[:, g * T + half * 256:g * T + half * 256 + 256], start=True, stop=True))
            return out_

        def hat_abs(s, c, slot):
            r0, r1 = chunks[c]
            n = (r1 - r0) * 256
            src = psum[:, 2 * slot:2 * slot + 2, :].rearrange("p a n -> p (a n)")[:, 0:n]
            return ae.activation(hat[:, s, r0:r1, :].rearrange("p r n -> p (r n)"), src, ACT.Abs,
                                 bias=cols[:, C_NEGP:C_NEGP + 1])

        def hat_low(s, c):
            w = hat[:, s, chunks[c][0]:chunks[c][1], :]
            return ve.tensor_scalar(w, w, 1.0, 1.0, ALU.min, ALU.subtract)

        def sampled(t, half, bb, s, g):
            b = 4 * half + bb
            out_ = []
            for i in range(2):
                h = 2 * t + i
                out_.append(lambda i=i, h=h: pe.matmul(
                    psum[64 * i:64 * i + 64, g, 0:320], kv[:, b, h * 64:(h + 1) * 64],
                    hat[:, s, 5 * i:5 * i + 5, bb * S:(bb + 1) * S], start=True, stop=True))
            return out_

        def weighed(out_, t, b, g):
            return ve.tensor_tensor(out_.rearrange("p (k q) -> p k q", k=NK),
                                    psum[:, g, 0:320].rearrange("p (k q) -> p k q", k=NK),
                                    qm[:, t, b * S:(b + 1) * S].unsqueeze(1).broadcast_to([P, NK, S]), ALU.mult)

        def pe_spread(n, c):
            t, half = units[n]
            x = 3 * n + c
            fns = spread(t, half, c, x % 2)
            w = ("v.pos.rp", "d.sel", "v.flag") + ((f"a.hat{x - 2}",) if x >= 2 else ("a.l1.xt3", "v.l1.xt2"))
            for i, fn in enumerate(fns):
                PE.do(fn, f"sp{x}" if i == len(fns) - 1 else None, w)

        def pe_sample(n, bbs):
            t, half = units[n]
            for bb in bbs:
                y = 4 * n + bb
                w = (f"v.low{3 * n + 2}", "v.kv15") + ((f"v.g{y - 4}",) if y >= 4 else ())
                fns = sampled(t, half, bb, n % 2, 4 + y % 4)
                for i, fn in enumerate(fns):
                    PE.do(fn, f"g{y}" if i == 1 else None, w)

        NU = len(units)
        for n in range(NU + 1):
            if n < NU:
                for c in range(3):
                    if c == 2 and n:
                        pe_sample(n - 1, (0, 1))
                    pe_spread(n, c)
                    x = 3 * n + c
                    A.do(lambda n=n, c=c, x=x: hat_abs(n % 2, c, x % 2), f"hat{x}",
                         (f"p.sp{x}",) + ((f"p.g{4 * (n - 2) + 3}",) if n >= 2 else ("v.flag",)))
                    vi(lambda n=n, c=c: hat_low(n % 2, c), f"low{x}", (f"a.hat{x}",))
            if n >= 1:
                pe_sample(n - 1, (2, 3) if n < NU else range(4))
                t, half = units[n - 1]
                for bb in range(4):
                    y = 4 * (n - 1) + bb
                    b = 4 * half + bb
                    vi(lambda t=t, b=b, y=y: weighed(acc[:, t * 8 + b, :], t, b, 4 + y % 4), f"g{y}",
                       (f"p.g{y}", "a.qm15"))

        g_d, g_kvp, g_kvv, g_rp, g_sp, g_hat, g_low, g_gp, g_gv, g_arr = (
            sem("g_" + n) for n in ("d", "kvp", "kvv", "rp", "sp", "hat", "low", "gp", "gv", "arr"))
        g_go = {e: sem("g_go" + e) for e in "vap"}
        g_all = [g_d, g_kvp, g_kvv, g_rp, g_sp, g_hat, g_low, g_gp, g_gv, g_arr]
        g_ini = sem("g_ini")

        def rest(eng, who, body, first=None, last=None):
            def run():
                val = eng.value_load(flagi[0:1, 0:1], min_val=0, max_val=1)
                with eng.If(val):
                    if first:
                        first()
                    with eng.Fori(1, NB) as j:
                        body(j)
                        if who != "s":
                            eng.sem_inc(g_arr, 1)
                            eng.wait_ge(g_go[who], 1)
                            eng.sem_clear(g_go[who])
                        else:
                            eng.wait_ge(g_arr, 3)
                            for s in g_all:
                                eng.sem_clear(s)
                            for s in g_go.values():
                                eng.sem_inc(s, 1)
            return run

        def rest_sp(j):
            sp.dma_start(ctx_r[:, :], io["ctx"].rearrange("j p b k m -> j p (b k m)")[bass.DynSlice(j, 1), :, :]
                         .rearrange("a p n -> (a p) n")).then_inc(g_d, 16)
            sp.dma_start(vcol[:, :], io["vld"][bass.DynSlice(j, 1), :, :].rearrange("a p n -> (a p) n")).then_inc(g_d, 16)
            sp.wait_ge(g_d, 32)

        def rest_v(j):
            ve.tensor_scalar(t1g, ix[:, :], 66.0, -66.0, ALU.min, ALU.max).then_inc(g_rp, 1)
            ve.wait_ge(g_rp, 1)
            ve.tensor_copy(rp[:, :], t1g).then_inc(g_rp, 1)
            ve.wait_ge(g_rp, 2)
            ve.tensor_tensor(rp[64:104, :], t1g[64:104, :], rp[64:104, :], ALU.subtract).then_inc(g_rp, 1)
            ve.wait_ge(g_rp, 3)
            ve.tensor_scalar(ix[:, :], ix[:, :], -128.0, None, ALU.add).then_inc(g_rp, 1)
            ve.wait_ge(g_rp, 4)
            ve.wait_ge(g_d, 32)
            for j2 in range(16):
                b, half = j2 // 2, j2 % 2
                ve.wait_ge(g_kvp, j2 + 1)
                ve.scalar_tensor_tensor(out=kv[:, b, half * D:(half + 1) * D], in0=bkv[:, half * D:(half + 1) * D],
                                        scalar=vcol[:, 0:1], in1=bank(4 + j2 % 4), op0=ALU.mult,
                                        op1=ALU.add).then_inc(g_kvv, 1)
            for n in range(NU):
                t, half = units[n]
                for c in range(3):
                    ve.wait_ge(g_hat, 3 * n + c + 1)
                    hat_low(0, c).then_inc(g_low, 1)
                for bb in range(4):
                    y = 4 * n + bb
                    b = 4 * half + bb
                    ve.wait_ge(g_gp, y + 1)
                    weighed(tmpg[:, :], t, b, 4 + y % 4).then_inc(g_gv, 1)
                    ve.wait_ge(g_gv, 2 * y + 1)
                    ve.tensor_tensor(acc[:, t * 8 + b, :], acc[:, t * 8 + b, :], tmpg[:, :], ALU.add).then_inc(g_gv, 1)
                    ve.wait_ge(g_gv, 2 * y + 2)

        t1g = w_r[0:104, 2560:3584]

        def rest_v_first():
            ve.tensor_scalar(ix[:, :], ix[:, :], float(DEAD + 1 - P - 64), None, ALU.add).then_inc(g_ini, 1)
            ve.wait_ge(g_ini, 1)

        def rest_a(j):
            for n in range(NU):
                for c in range(3):
                    x = 3 * n + c
                    ae.wait_ge(g_sp, x + 1)
                    if n >= 1:
                        ae.wait_ge(g_gp, 4 * n)
                    hat_abs(0, c, x % 2).then_inc(g_hat, 1)

        def rest_p(j):
            pe.wait_ge(g_d, 32)
            for j2 in range(16):
                b, half = j2 // 2, j2 % 2
                if j2 >= 4:
                    pe.wait_ge(g_kvv, j2 - 3)
                for k in range(KC):
                    mm = pe.matmul(bank(4 + j2 % 4), ctxt[:, b, k, :], wkv[:, k, half * D:(half + 1) * D],
                                   start=(k == 0), stop=(k == KC - 1))
                mm.then_inc(g_kvp, 1)
            pe.wait_ge(g_rp, 3)
            pe.wait_ge(g_kvv, 16)
            for n in range(NU):
                t, half = units[n]
                for c in range(3):
                    x = 3 * n + c
                    if x >= 2:
                        pe.wait_ge(g_hat, x - 1)
                    for fn in spread(t, half, c, x % 2):
                        mm = fn()
                    mm.then_inc(g_sp, 1)
                pe.wait_ge(g_low, 3 * n + 3)
                for bb in range(4):
                    y = 4 * n + bb
                    if y >= 4:
                        pe.wait_ge(g_gv, 2 * (y - 3))
                    for fn in sampled(t, half, bb, 0, 4 + y % 4):
                        mm = fn()
                    mm.then_inc(g_gp, 1)

        first_done = ("v.g63", "p.g63", "v.flag")
        SP.do(rest(sp, "s", rest_sp), wait=first_done)
        V.do(rest(ve, "v", rest_v, first=rest_v_first), wait=first_done)
        A.do(rest(ae, "a", rest_a), wait=first_done)
        PE.do(rest(pe, "p", rest_p), wait=first_done)
        vi(lambda: ve.memset(small[0:1, 40:41], 0.0), "rest")

        free = ("v.rest",)
        load("bsel", bsel, io["bsel"], free)
        load("wo", wo, io["wo"], free)
        load("x2", xr, io["x"].rearrange("(m p) d -> p m d", p=P), free)
        load("rows", rowt, io["rows"].unsqueeze(0).broadcast_to([P, 3, D]), free)
        load("wb", wb, io["wb"], free)
        load("wc", wc, io["wc"], free)
        load("wd", wd, io["wd"], free)

        def add_row(r, dst, wait):
            vi(lambda: ve.tensor_tensor(dst, dst, rowt[:, r, :].unsqueeze(1).broadcast_to([P, NT, D]), ALU.add),
               f"row{r}", wait)

        for w in range(32):
            for o in range(2):
                PE.do(lambda w=w, o=o: pe.matmul(psum[64 * o:64 * o + 64, w // 16, 0:320],
                                                 zsel[:, o, 62 - 2 * w:126 - 2 * w],
                                                 acc[:, 16 * (w // 8) + w % 8 + 8 * o, :],
                                                 start=(w % 16 == 0), stop=(w % 16 == 15)),
                      f"score{w // 8}" if w % 8 == 7 and o else None, ("v.rest", "d.zsel", "a.hat47"))
        def join(j):
            for base, q, who in ((0, A, ae), (64, V, ve)):
                def run(base=base, who=who):
                    dst = acc_r[base:base + 32, 5120 * j:5120 * j + 2560]
                    src = acc_r[base:base + 32, 5120 * j + 2560:5120 * j + 5120]
                    return who.tensor_copy(dst, src) if who is ve else who.activation(dst, src, ACT.Copy)
                q.do(run, f"join{j}", (f"p.score{j}",))

        def kq(ap):
            return ap.rearrange("p (k q) -> p k q", k=NK)

        def qk(ap):
            return ap.rearrange("p (k q) -> p q k", k=NK)

        def over_k(ap):
            return ap.unsqueeze(1).broadcast_to([P, NK, S])

        def softmax(g):
            o = 1024 * g
            sc, ex, mn, sm, rc = (w_r[:, o + a:o + b] for a, b in ((0, 320), (320, 640), (640, 704), (704, 768),
                                                                   (768, 832)))
            hi, lo = w_r[:, o + 832:o + 992].bitcast(F16), sc[:, 0:160].bitcast(F16)
            raw = psum[:, g, 0:320]
            v(lambda: ve.tensor_reduce(mn, qk(raw), AX.X, ALU.min), None, (f"p.score{2 * g + 1}",))
            v(lambda: ve.tensor_tensor(kq(sc), kq(raw), over_k(mn), ALU.subtract), f"sc{g}")
            A.do(lambda: ae.activation(ex, sc, ACT.Exp, scale=-0.5 / HD ** 0.5), f"ex{g}", (f"v.sc{g}",))
            v(lambda: ve.tensor_reduce(sm, qk(ex), AX.X, ALU.add), None, (f"a.ex{g}",))
            v(lambda: ve.reciprocal(rc, sm))
            v(lambda: ve.tensor_scalar(rc, rc, -0.5, None, ALU.mult))
            v(lambda: ve.tensor_tensor(kq(ex), kq(ex), over_k(rc), ALU.mult))
            v(lambda: ve.tensor_copy(hi, ex), f"ahi{g}")
            v(lambda: ve.tensor_tensor(lo, ex, hi, ALU.subtract), f"at{g}")
            return hi, lo

        def av(w, halves):
            g, u = w // 16, 16 * (w // 8) + w % 8
            for i, a in enumerate(halves):
                PE.do(lambda i=i, a=a: pe.matmul(psum[:, 4 + w % 4, 0:320], bsel[:, w, :], a, start=(i == 0),
                                                 stop=(i == 1)), f"av{w}" if i else None,
                      (f"v.at{g}", "d.bsel") + ((f"v.av{w - 4}",) if w >= 4 else ()))
            vi(lambda: ve.tensor_tensor(acc[:, u, :], acc[:, u, :], psum[:, 4 + w % 4, 0:320], ALU.mult),
               f"av{w}", (f"p.av{w}", f"a.join{w // 8}", f"v.join{w // 8}"))
            if w % 4 == 3:
                dst = wkv_r[:, (w - 3) * S:(w + 1) * S].rearrange("p (u q) -> p u q", u=4)
                part_ = [acc[:, u - 3:u + 1, k * S:(k + 1) * S] for k in range(NK)]
                if w in POOL:
                    for k in range(1, NK):
                        a = part_[0] if k == 1 else dst
                        GP.do(lambda a=a, k=k: gp.tensor_tensor(dst, a, part_[k], ALU.add), f"ctx{w}.{k}",
                              (f"v.av{w}",) + ((f"g.{GP.last}",) if GP.last else ()))
                else:
                    v(lambda: ve.tensor_reduce(dst, acc[:, u - 3:u + 1, :].rearrange("p u (k q) -> p u q k", k=NK),
                                               AX.X, ALU.add), f"ctx{w}")

        POOL = (3, 7, 11, 15, 19, 23)
        join(0)
        join(1)
        halves = [softmax(0)]
        join(2)
        for w in range(4):
            av(w, halves[0])
        halves.append(softmax(1))
        join(3)
        GP.do(lambda: gp.tensor_tensor(xr, xr, rowt[:, 0, :].unsqueeze(1).broadcast_to([P, NT, D]), ALU.add), "row0",
              (f"g.{GP.last}", "d.x2", "d.rows"))

        def out_chunk(k):
            for m in range(NT):
                PE.do(lambda m=m: pe.matmul(bank(m), ctxp[:, k, m * P:(m + 1) * P], wo[:, k, :], start=(k == 0),
                                            stop=(k == 3)), f"o{m}" if k == 3 else None,
                      (f"v.at1", "d.wo") + tuple(f"g.ctx{w}.4" if w in POOL else f"v.ctx{w}"
                                                 for w in (8 * k + 3, 8 * k + 7)))

        for w in range(4, 32):
            av(w, halves[w // 16])
            if w % 8 == 7 and w > 8:
                out_chunk(w // 8 - 1)
        out_chunk(3)

        A.do(lambda: ae.activation(dtc, cols[:, C_DT:C_DT + 1], ACT.Exp), "dt", ("d.cols",))
        A.do(lambda: ae.activation(abar, cols[:, C_LOGA:C_LOGA + 4], ACT.Exp), "ea", ("v.rest",))
        v(lambda: ve.tensor_scalar(abar, abar, dtc, -1.0, ALU.mult, ALU.mult), "adt", ("a.dt", "a.ea"))
        A.do(lambda: ae.activation(abar, abar, ACT.Exp), "abar", ("v.adt",))
        for m in range(NT):
            v(lambda m=m: ve.tensor_tensor(xr[:, m, :], xr[:, m, :], bank(m), ALU.add), f"x1.{m}", (f"p.o{m}", "g.row0"))
            stats("l2", xr, m, (f"v.x1.{m}",))
            normalise("l2", xr, xn2, m)
            if m:
                transposes("l2", xn2, 4, m - 1, ("v.av31",))
        transposes("l2", xn2, 4, NT - 1)
        transposed("l2", xt2, 4)

        for k in range(KC):
            v(lambda k=k: ve.tensor_copy(coef[:, k, :], abar[:, k:k + 1].broadcast_to([P, T])), None, ("a.abar",))
        v(lambda: ve.memset(coef.rearrange("p k (b t) -> p k b t", b=B)[:, :, :, 0:1], 0.0), "coef")
        for m in range(4):
            product(bank(m), lambda k, m=m: wb[:, k, m * P:(m + 1) * P], lambda k: xt2[:, k, :], KC, f"bu{m}",
                    ("a.l2.xt3", "v.l2.xt2", "d.wb", "v.x1.3"))
            v(lambda m=m: ve.tensor_scalar(bu[:, m, :], bank(m), cols[:, C_BB + m:C_BB + m + 1], dtc, ALU.add,
                                           ALU.mult), f"bu{m}", (f"p.bu{m}",))
            v(lambda m=m: ve.tensor_tensor_scan(xs[:, m, :], coef[:, m, :], bu[:, m, :], 0.0, ALU.mult, ALU.add),
              f"xs{m}")
        add_row(1, xr, ("v.l2.xn3",))
        add_row(2, xr, ("v.row1",))
        for m in range(NT):
            for i in range(2 * KC):
                lhs, w, k = (xt2, wd, i) if i < KC else (xs, wc, i - KC)
                PE.do(lambda m=m, i=i, lhs=lhs, w=w, k=k: pe.matmul(
                    bank(4 + m), lhs[:, k, m * P:(m + 1) * P], w[:, k, :], start=(i == 0), stop=(i == 7)),
                    f"y{m}" if i == 7 else None, ("d.wd", "d.wc") if i < KC else (f"v.xs{k}",))
            v(lambda m=m: ve.tensor_tensor(xr[:, m, :], xr[:, m, :], bank(4 + m), ALU.add), f"x2.{m}", (f"p.y{m}",))
            stats("l3", xr, m, (f"v.x2.{m}",))
            normalise("l3", xr, xn3, m)
            if m:
                transposes("l3", xn3, 0, m - 1, ("v.bu3",))
        transposes("l3", xn3, 0, NT - 1)
        transposed("l3", xt3, 0)

        NE = E - 1
        (p_lo, p_hi, p_list, p_turn, p_gate, p_down, v_first, v_pick, v_list, v_pad, v_rows, v_xg, v_hid, a_xg, a_silu,
         a_turn, a_y, g_dma, g_sum, g_turn, g_end) = (sem("t_" + n) for n in (
             "pl", "ph", "ps", "pt", "pg", "pd", "vf", "vp", "vl", "va", "vr", "vx", "vh", "ax", "as", "at", "ay",
             "gd", "gs", "gt", "ge"))
        counts, now, this, base1, base2, now16 = {}, {}, {}, {}, {}, {}

        def prepare(eng, name, own=()):
            def run():
                regs = [eng.alloc_register(f"{name}_cnt{n}") for n in range(NE)]
                eng.reg_load(regs, cnt[0:1, 1:E])
                counts[eng] = [eng.snap(r, donate=True, min_val=0, max_val=T) for r in regs]
                for what, regs, value in (
                        ("now", now, 1), ("this", this, 2), ("b1", base1, 1), ("b2", base2, 1), ("n16", now16, 16)):
                    regs[eng] = eng.alloc_register(f"{name}_{what}")
                    eng.reg_mov(regs[eng], value)
                for s in own:
                    eng.sem_inc(s, 1)
            return run

        def pick(dst, n, i):
            for m in range(NT):
                c = m * E + n + 1
                op = ve.tensor_scalar(dst[:, m, :], iota[:, i * P:(i + 1) * P], posm[:, c:c + 1], None, ALU.is_equal)
            return op

        load("rw", rw, io["rw"], ("v.at1", "v.ctx31", "p.av31"))

        load("ltri", ltri, io["ltri"], ("p.y3",))
        load("iota", iota, io["iota"].broadcast_to([P, T]), ("p.y3",))
        for e in range(NW):
            w = wbufs[e % NW]
            wait = ("p.o3", "p.av31") if e < 2 else ("v.ctx31",)
            load(f"wgu{e}", w[:, 0:2048].rearrange("p (k n) -> p k n", k=KC), io["wgu"][e], wait)
            load(f"wdn{e}", w[:, 2048:3072].rearrange("p (i n) -> p i n", i=2), io["wdn"][e], wait)
        for m in range(NT):
            for k in range(KC):
                PE.do(lambda m=m, k=k: pe.matmul(psum[:, 4, m * E:(m + 1) * E], xt3[:, k, m * P:(m + 1) * P],
                                                 rw[:, k, :], start=(k == 0), stop=(k == 3)),
                      "route" if m == 3 and k == 3 else None, ("a.l3.xt3", "v.l3.xt2", "d.rw", "v.x2.3"))
        s0, s1, s2, s3 = rt
        scr = s0[:, 0:64]
        cho = s0[:, 64:128]
        prs = s0[:, 128:144 + 80]
        grp = s0[:, 256:272]
        gsel = s0[:, 272:288]
        mch = s0[:, 320:384]
        msel = s0[:, 384:448]
        wsum = s0[:, 448:452]
        A.do(lambda: ae.activation(scr, psum[:, 4, 0:64], ACT.Sigmoid), "scr", ("p.route", "v.xs3"))
        v(lambda: ve.tensor_tensor(cho.rearrange("p (m e) -> p m e", m=NT), scr.rearrange("p (m e) -> p m e", m=NT),
                                   rbt[:, :].unsqueeze(1).broadcast_to([P, NT, E]), ALU.add), None,
          ("a.scr", "d.rb", "p.y3"))
        c4 = cho.rearrange("p (g i) -> p g i", i=4)
        pr = s0[:, 128:224].rearrange("p (g j) -> p g j", j=6)
        v(lambda: ve.tensor_tensor(pr[:, :, 0:3], c4[:, :, 0:1].broadcast_to([P, 16, 3]), c4[:, :, 1:4], ALU.add))
        v(lambda: ve.tensor_tensor(pr[:, :, 3:5], c4[:, :, 1:2].broadcast_to([P, 16, 2]), c4[:, :, 2:4], ALU.add))
        v(lambda: ve.tensor_tensor(pr[:, :, 5:6], c4[:, :, 2:3], c4[:, :, 3:4], ALU.add))
        v(lambda: ve.tensor_reduce(grp, pr, AX.X, ALU.max))

        def ranked(val, n, rows, low, gt, ge, out_, keep):
            vv = val.rearrange("p (r i) -> p r i", i=n)
            other = vv.unsqueeze(2).broadcast_to([P, rows, n, n])
            mine = vv.unsqueeze(3).broadcast_to([P, rows, n, n])
            g4 = gt.rearrange("p (r i j) -> p r i j", r=rows, i=n)
            e4 = ge.rearrange("p (r i j) -> p r i j", r=rows, i=n)
            g3 = gt.rearrange("p (r c) -> p r c", r=rows)
            e3 = ge.rearrange("p (r c) -> p r c", r=rows)
            lw = low.unsqueeze(1).broadcast_to([P, rows, n * n])
            v(lambda: ve.tensor_tensor(g4, other, mine, ALU.is_gt))
            v(lambda: ve.tensor_tensor(e4, other, mine, ALU.is_equal))
            v(lambda: ve.tensor_tensor(e3, e3, lw, ALU.mult))
            v(lambda: ve.tensor_tensor(gt, gt, ge, ALU.add))
            v(lambda: ve.tensor_reduce(out_, g4, AX.X, ALU.add))
            v(lambda: ve.tensor_scalar(out_, out_, float(keep), None, ALU.is_lt))

        vi(lambda: ve.memset(small[:, 50:51], 0.0), "lowok", ("d.low",))
        ranked(grp, 4, NT, lowt[:, 0:16], s1[:, 0:64], s1[:, 64:128], gsel, 2)
        g3 = gsel.unsqueeze(2).broadcast_to([P, 16, 4])
        m3 = mch.rearrange("p (g i) -> p g i", i=4)
        v(lambda: ve.tensor_tensor(m3, c4, g3, ALU.mult))
        v(lambda: ve.tensor_scalar(gsel, gsel, 1.0, 1e9, ALU.subtract, ALU.mult))
        v(lambda: ve.tensor_tensor(m3, m3, g3, ALU.add))
        ranked(mch, E, NT, lowt[:, 16:272], s2, s3, msel, 4)
        sel0 = selc[:, 4, :]
        m3e = msel.rearrange("p (m e) -> p m e", m=NT)
        v(lambda: ve.memset(selc[:, 0, :], 0.0), None, ("p.y3", "p.bu3", "v.xs3"))
        for m in range(NT):
            v(lambda m=m: ve.tensor_tensor(selc[:, m + 1, :], selc[:, m, :], m3e[:, m, :], ALU.add),
              "selc" if m == NT - 1 else None)
        def weights(e):
            w = wbufs[e % NW]
            return w[:, 0:2048].rearrange("p (k n) -> p k n", k=KC), w[:, 2048:3072].rearrange("p (i n) -> p i n", i=2)

        A.do(lambda: ae.activation(xh.rearrange("p m d -> p (m d)"), xn3.rearrange("p m d -> p (m d)"), ACT.Copy),
             "xh", ("v.l3.xn3", "p.y3"))
        v(lambda: ve.tensor_tensor(xl.rearrange("p m d -> p (m d)"), xn3.rearrange("p m d -> p (m d)"),
                                   xh.rearrange("p m d -> p (m d)"), ALU.subtract), "xl", ("a.xh", "p.y3"))
        gu0, dn0 = weights(0)
        for i in range(4):
            product(bank(i), lambda k, i=i: gu0[:, k, i * P:(i + 1) * P], lambda k: xt3[:, k, :], KC, f"gu0.{i}",
                    ("d.wgu0", "a.l3.xt3", "v.l3.xt2"))
        A.do(lambda: ae.activation(silu0, psum[:, 0:2, :].rearrange("p a n -> p (a n)"), ACT.Silu), "si0",
             ("p.gu0.1", "p.y3"))
        v(lambda: ve.tensor_tensor(hid0.rearrange("p i n -> p (i n)"), silu0,
                                   psum[:, 2:4, :].rearrange("p a n -> p (a n)"), ALU.mult), "h0",
          ("a.si0", "p.gu0.3"))
        PE.do(lambda: pe.matmul(psum[:, 4, 64:128], ltri, msel, start=True, stop=False), None, ("v.selc", "d.ltri"))
        PE.do(lambda: pe.matmul(psum[:, 4, 64:128], ones[:, :], selc[:, 0:4, :].rearrange("p m e -> p (m e)"),
                                start=False, stop=True))
        PE.do(lambda: pe.matmul(psum[:, 5, 0:E], ones[:, :], sel0, start=True, stop=True), "before")
        v(lambda: ve.scalar_tensor_tensor(out=posm, in0=psum[:, 4, 64:128], scalar=1.0, in1=msel, op0=ALU.add,
                                          op1=ALU.mult), None, ("p.before",))
        v(lambda: ve.tensor_scalar(posm, posm, -1.0, None, ALU.add), "pos")
        v(lambda: ve.tensor_copy(cnt[0:1, :], psum[0:1, 5, 0:E]), "cnt")
        vi(lambda: pick(picks[2], 0, 0), "pick0", ("d.iota", "v.pos"))
        V.do(lambda: ve.sem_inc(v_first, 1), wait=("v.pick0",))
        ready = ("v.cnt",)
        SP.do(prepare(sp, "s"), wait=ready)
        GP.do(prepare(gp, "g", [g_sum]), wait=ready)
        v(lambda: ve.tensor_tensor(msel, msel, scr, ALU.mult))
        v(lambda: ve.tensor_reduce(wsum, msel.rearrange("p (m e) -> p m e", m=NT), AX.X, ALU.add))
        v(lambda: ve.tensor_scalar(wsum, wsum, 1e-20, None, ALU.add))
        v(lambda: ve.reciprocal(wsum, wsum))
        v(lambda: ve.tensor_scalar(wsum, wsum, 2.5, None, ALU.mult))
        v(lambda: ve.tensor_tensor(comb[:, :, :], m3e, wsum.unsqueeze(2).broadcast_to([P, NT, E]), ALU.mult), "comb")
        v(lambda: ve.memset(rh[:, :, :, 3:4], 0.0))
        v(lambda: ve.tensor_copy(rh[:, :, :, 0], tokc[:, 0:NT].unsqueeze(2).broadcast_to([P, NT, E])), None,
          ("d.tokc",))
        V.do(prepare(ve, "v", [v_pick, v_list, v_pad, v_rows, v_xg, v_hid]), wait=ready)
        A.do(prepare(ae, "a", [a_xg, a_silu, a_turn, a_y]), wait=ready)
        for m in range(NT):
            if m == 2:
                PE.do(prepare(pe, "p", [p_lo, p_hi, p_list, p_turn, p_gate, p_down]), wait=ready)
            product(bank((6, 7, 4, 5)[m]), lambda k, m=m: hid0[:, k, m * P:(m + 1) * P], lambda k: dn0[:, k, :], 2,
                    f"gd0.{m}", ("d.wdn0", "v.h0", "a.scr") + (("v.cnt",) if m >= 2 else ()))
            vi(lambda m=m: ve.scalar_tensor_tensor(out=xr[:, m, :], in0=bank((6, 7, 4, 5)[m]),
                                                   scalar=comb[:, m, 0:1], in1=xr[:, m, :], op0=ALU.mult,
                                                   op1=ALU.add), f"x3.{m}", (f"p.gd0.{m}", "v.comb"))
        v(lambda: ve.tensor_copy(rh[:, :, :, 1], comb[:, :, :]))
        v(lambda: ve.tensor_tensor(rh[:, :, :, 2], comb[:, :, :], rh[:, :, :, 1], ALU.subtract), "rh")

        def tiles(eng, tile, empty=None, tail=None, start=None, end=None):
            def run():
                c = counts[eng]

                def before(n, fn):
                    if n:
                        with eng.If(c[n - 1] > 0):
                            fn()

                for n in range(NE):
                    if start:
                        start(n)

                    def level(i):
                        if i == NT:
                            if tail:
                                tail(n, NT - 1)
                            return
                        with eng.If(c[n] > P * i):
                            tile(n, i, before)
                            eng.reg_add(now[eng], now[eng], 1)
                            eng.reg_add(this[eng], this[eng], 1)
                            level(i + 1)
                        if i and tail:
                            with eng.Else():
                                tail(n, i - 1)
                        if not i and empty:
                            with eng.Else():
                                empty(n, before)
                    level(0)
                if end:
                    before(NE, end)
            return run

        def pe_turn():
            pe.wait_ge(v_hid, now[pe])
            for c in range(2):
                tr = pe.transpose(psum[:, 2, c * P:(c + 1) * P], hid[:, c * P:(c + 1) * P], ident[:, :])
            tr.then_inc(p_turn, 1)

        def pe_down(n):
            dn = weights(n + 1)[1]
            pe.wait_ge(dsem[f"wdn{n + 1}"], 16)
            pe.wait_ge(a_turn, now[pe])
            for c in range(2):
                mm = pe.matmul(bank(4), hidt[:, c * P:(c + 1) * P], dn[:, c, :], start=(c == 0), stop=(c == 1))
            mm.then_inc(p_down, 1)

        def pe_both(n):
            pe_turn()
            pe_down(n)

        def pe_tile(n, i, before):
            if i:
                pk = picks[i % 2]
                pe.wait_ge(v_pick, now[pe])
            else:
                pk = picks[2 + n % 2]
                pe.wait_ge(v_first, n + 1)
            pe.wait_ge(v_xg, now[pe])
            pe.wait_ge(a_xg, now[pe])
            for k in range(KC):
                for j, part_ in enumerate((xh, xl)):
                    for m in range(NT):
                        mm = pe.matmul(psum[:, 5 * (k // 2), (k % 2) * P:(k % 2 + 1) * P],
                                       part_[:, m, k * P:(k + 1) * P], pk[:, m, :],
                                       start=(j == 0 and m == 0), stop=(j == 1 and m == NT - 1))
                if k % 2:
                    mm.then_inc(p_hi if k == 3 else p_lo, 1)
            pe.wait_ge(v_list, now[pe])
            for m in range(NT):
                mm = pe.matmul(psum[:, 1, 0:4], pk[:, m, :], rh[:, m, n + 1, :], start=(m == 0), stop=(m == NT - 1))
            mm.then_inc(p_list, 1)
            if i:
                pe_turn()
            else:
                before(n, pe_turn)
            gu, _ = weights(n + 1)
            pe.wait_ge(dsem[f"wgu{n + 1}"], 16)
            pe.wait_ge(a_xg, this[pe])
            for k in range(KC):
                if k == 2:
                    pe.wait_ge(v_xg, this[pe])
                mm = pe.matmul(bank(3), xg[:, k * P:(k + 1) * P], gu[:, k, :], start=(k == 0), stop=(k == KC - 1))
            mm.then_inc(p_gate, 1)
            if i:
                pe_down(n)
            else:
                before(n, lambda: pe_down(n - 1))

        def pick_first(n):
            if n < NE:
                ve.wait_ge(v_first, n)
                pick(picks[2 + n % 2], n, 0).then_inc(v_first, 1)

        def v_tile(n, i, before):
            ve.wait_ge(p_hi, this[ve])
            ve.wait_ge(p_gate, now[ve])
            ve.tensor_copy(xg[:, 256:512], psum[:, 5, 0:256]).then_inc(v_xg, 1)
            ve.wait_ge(p_list, this[ve])
            ve.wait_ge(v_rows, now[ve])
            ve.tensor_copy(lst, psum[:, 1, 0:4]).then_inc(v_list, 1)
            ve.wait_ge(v_list, this[ve])
            ve.wait_ge(v_hid, now[ve])
            ve.tensor_tensor(wcol, lst[:, 1:2], lst[:, 2:3], ALU.add)
            ve.tensor_scalar(pad, lst[:, 0:1], 0.0, tokc[:, 4:5], ALU.is_equal, ALU.mult).then_inc(v_pad, 1)
            if i == 0:
                pick_first(n + 1)
            ve.wait_ge(v_pad, this[ve])
            t = NT * n + i
            ve.scalar_tensor_tensor(out=slot_rows[:, t:t + 1], in0=lst[:, 0:1], scalar=-1.0, in1=pad, op0=ALU.add,
                                    op1=ALU.add).then_inc(v_rows, 1)
            if i < NT - 1:
                ve.wait_ge(v_pick, now[ve])
                pick(picks[(i + 1) % 2], n, i + 1).then_inc(v_pick, 1)
            else:
                ve.wait_ge(v_pick, now[ve])
                ve.sem_inc(v_pick, 1)
            ve.wait_ge(a_silu, this[ve])
            ve.wait_ge(p_turn, now[ve])
            ve.scalar_tensor_tensor(out=hid, in0=silu, scalar=wcol, in1=psum[:, 3, 256:512], op0=ALU.mult,
                                    op1=ALU.mult).then_inc(v_hid, 1)

        def v_empty(n, before):
            if n + 1 < NE:
                ve.wait_ge(p_list, now[ve])
                pick_first(n + 1)

        def a_turned():
            ae.wait_ge(p_turn, now[ae])
            ae.activation(hidt, psum[:, 2, 0:256], ACT.Copy).then_inc(a_turn, 1)

        def a_down(n, i):
            ae.wait_ge(p_down, now[ae])
            if i == 0:
                y, ready = ys[6 + (n - 1) % 4], base2
            else:
                y, ready = ys[3 * (n % 2) + i - 1], base1
            ae.wait_ge(g_sum, ready[ae])
            ae.activation(y, bank(4), ACT.Copy).then_inc(a_y, 1)

        def a_both(n):
            a_turned()
            a_down(n + 1, 0)

        a_at = {}

        def a_start(n):
            if n == 0:
                a_at[0] = ae.alloc_register("a_at")
                ae.reg_mov(a_at[0], 1)
            ae.reg_mov(base2[ae], base1[ae])
            ae.reg_mov(base1[ae], a_at[0])
            ae.reg_mov(a_at[0], now[ae])

        def a_tile(n, i, before):
            ae.wait_ge(p_lo, this[ae])
            ae.wait_ge(p_gate, now[ae])
            ae.activation(xg[:, 0:256], psum[:, 0, 0:256], ACT.Copy).then_inc(a_xg, 1)
            if i:
                a_turned()
            else:
                before(n, a_turned)
            ae.wait_ge(p_gate, this[ae])
            ae.wait_ge(v_hid, now[ae])
            ae.activation(silu, psum[:, 3, 0:256], ACT.Silu).then_inc(a_silu, 1)
            if i:
                a_down(n, i)
            else:
                before(n, lambda: a_down(n, 0))

        def g_scatter(y, n, i):
            j = NT * n + i
            gp.sem_inc(g_turn, 1)
            gp.indirect_dma_start(out, bass.IndirectOffsetOnAxis(slot_rows[:, j:j + 1].bitcast(mybir.dt.uint32), 0),
                                  y, None, bounds_check=T + P - 1, oob_is_err=True,
                                  compute_op=ALU.add).then_inc(g_dma, 16)
            gp.wait_ge(g_dma, now16[gp])
            gp.sem_inc(g_sum, 1)
            gp.reg_add(now16[gp], now16[gp], 16)

        def g_tile(n, i, before):
            if i:
                gp.wait_ge(a_y, now[gp])
                gp.wait_ge(v_rows, now[gp])
                g_scatter(ys[3 * (n % 2) + i - 1], n, i - 1)

        def g_tail(n, last):
            gp.wait_ge(a_y, now[gp])
            gp.wait_ge(v_rows, now[gp])
            g_scatter(ys[6 + n % 4], n, last)

        for m in range(NT):
            SP.do(lambda m=m: sp.dma_start(out.rearrange("(m p) d -> p m d", p=P)[:, m, :], xr[:, m, :])
                  .then_inc(s_out, 16), wait=(f"v.x3.{m}",))
        SP.do(lambda: sp.dma_start(out.rearrange("(m p) d -> p m d", p=P)[:, NT, :], xr[:, 0, :])
              .then_inc(s_out, 16))
        def load_weights(e, wait=()):
            w = wbufs[e % NW]
            load(f"wgu{e}", w[:, 0:2048].rearrange("p (k n) -> p k n", k=KC), io["wgu"][e], wait)
            load(f"wdn{e}", w[:, 2048:3072].rearrange("p (i n) -> p i n", i=2), io["wdn"][e], wait)

        load_weights(NW, ("p.gd0.3",))
        for e in range(NW + 1, E):
            for name in ("wgu", "wdn"):
                dsem[f"{name}{e}"] = sem(f"d_{name}{e}")

        def s_start(n):
            e = n + NW
            if n and e < E:
                w = wbufs[e % NW]
                sp.wait_ge(p_down, now[sp])
                sp.wait_ge(dsem[f"wgu{n}"], 16)
                sp.wait_ge(dsem[f"wdn{n}"], 16)
                sp.dma_start(w[:, 0:2048].rearrange("p (k n) -> p k n", k=KC), io["wgu"][e]).then_inc(
                    dsem[f"wgu{e}"], 16)
                sp.dma_start(w[:, 2048:3072].rearrange("p (i n) -> p i n", i=2), io["wdn"][e]).then_inc(
                    dsem[f"wdn{e}"], 16)


        V.do(tiles(ve, v_tile, empty=v_empty))
        A.do(tiles(ae, a_tile, empty=lambda n, before: before(n, lambda: a_both(n - 1)), start=a_start,
                   end=lambda: a_both(NE - 1)), wait=("v.pick0", "v.xl", "v.rh"))
        PE.do(tiles(pe, pe_tile, empty=lambda n, before: before(n, lambda: pe_both(n - 1)),
                    end=lambda: pe_both(NE - 1)), wait=("v.pick0", "v.xl", "v.x3.3", "v.rh"))
        GP.do(lambda: gp.wait_ge(s_out, 16 * (NT + 1)))
        GP.do(tiles(gp, g_tile, tail=g_tail))
        GP.do(lambda: gp.sem_inc(g_end, 1))
        SP.do(tiles(sp, lambda n, i, before: None, start=s_start))
        SP.do(lambda: sp.wait_ge(s_out, 16 * (NT + 1)))
        SP.do(lambda: sp.wait_ge(g_end, 1))
        SP.do(lambda: None, wait=[f"d.{w}{e}" for e in range(E - NW, E) for w in ("wgu", "wdn")])

        block = ctx.enter_context(nc.Block())

        @block.sync
        def _(eng):
            emit(SP, eng, Q, dsem)

        @block.vector
        def _(eng):
            emit(V, eng, Q, dsem)

        @block.scalar
        def _(eng):
            emit(A, eng, Q, dsem)

        @block.tensor
        def _(eng):
            emit(PE, eng, Q, dsem)

        @block.gpsimd
        def _(eng):
            emit(GP, eng, Q, dsem)


def laid_out(a):
    def kt(w):
        return np.ascontiguousarray(w.T.reshape(KC, P, w.shape[0]).transpose(1, 0, 2))

    f = np.float32
    c = a["ctx_1024"]
    ring = np.zeros((B, NB * P, D), c.dtype)
    ring[:, 0:DEAD] = c[:, M - DEAD:]
    ring[:, DEAD + 1:M + 1] = c[:, :M - DEAD]
    ctx = ring.reshape(B, NB, P, KC, P).transpose(1, 4, 0, 3, 2)
    mask = np.zeros((B, P * 13), a["mask_BxS2_if0"].dtype)
    mask[:, :M] = a["mask_BxS2_if0"]
    wk, wv = a["L0_xattn_Wk"], a["L0_xattn_Wv"]
    order = np.stack([np.arange(D).reshape(H, HD), D + np.arange(D).reshape(H, HD)], 1)
    odd = np.arange(H) // 2 % 2 == 1
    order[odd] = order[odd][:, ::-1]
    order = order.ravel()
    wkv = np.concatenate([wk, wv])[order]
    bkv = np.concatenate([a["L0_xattn_bk"], a["L0_xattn_bv"]])[order][None]
    woff = np.zeros((2, 104, D), f)
    boff = np.zeros((2, 104), f)
    ref = np.zeros((2, 104), f)
    for g in range(2):
        for o in (0, 64):
            woff[g, o:o + 40] = a["L0_xattn_Woff"][40 * g:40 * g + 40]
            boff[g, o:o + 40] = a["L0_xattn_boff"][40 * g:40 * g + 40]
            ref[g, o:o + 40] = np.tile(np.arange(NK) - 3, 8)
    cols = np.zeros((P, C_N), f)
    cols[0:104, C_BOFF:C_BOFF + 2] = boff.T
    cols[0:104, C_REF:C_REF + 2] = ref.T
    cols[:, C_BQ:C_BQ + 4] = a["L0_xattn_bq"].reshape(4, P).T
    cols[:, C_BB:C_BB + 4] = a["L0_attn_b_B"].reshape(4, P).T
    cols[:, C_LOGA:C_LOGA + 4] = a["L0_attn_log_A"].reshape(4, P).T
    cols[:, C_DT] = a["L0_attn_log_dt"][0]
    p = np.arange(P)
    row = np.arange(NB * P).reshape(NB, P, 1)
    vld = ((row != DEAD) & (row <= M)).astype(f)
    cols[:, C_VLD] = vld[0, :, 0]
    cols[:, C_NEGP] = 64 - p
    sel = np.zeros((104, 40), np.float16)
    sel[np.arange(40), np.arange(40)] = 1
    sel[64 + np.arange(40), np.arange(40)] = 1
    zsel = np.zeros((P, 2, 126), f)
    for o in range(2):
        zsel[32 * o:32 * o + 32, o, 62] = 1
        zsel[64 + 32 * o:96 + 32 * o, o, 63] = 1
    bsel = np.zeros((P, 32, P), np.float16)
    wo = np.zeros((P, 4, D), f)
    wot = a["L0_xattn_Wo"].T.reshape(4, 4, HD, D)
    for i, at in enumerate((32, 96, 0, 64)):
        wo[at:at + 32] = wot[:, i].transpose(1, 0, 2)
        for w in range(32):
            bsel[64 * (i // 2) + 2 * w + i % 2, w, at:at + 32] = 1
    low4 = (np.arange(4)[None, :] < np.arange(4)[:, None]).astype(f)
    low16 = (np.arange(16)[None, :] < np.arange(16)[:, None]).astype(f)
    wg, wu = a["L0_ffn_w_gate"], a["L0_ffn_w_up"]
    wgu = np.concatenate([wg, wu], 1).transpose(0, 2, 1).reshape(E, KC, P, 2 * I).transpose(0, 2, 1, 3)
    wdn = a["L0_ffn_w_down"].transpose(0, 2, 1).reshape(E, 2, P, D).transpose(0, 2, 1, 3)
    return {
        "x": a["x"].reshape(T, D), "ctx": ctx, "mask": mask.reshape(B, P, 13).transpose(1, 0, 2), "wkv": kt(wkv),
        "bkv": bkv, "wq": kt(a["L0_xattn_Wq"]),
        "woff": woff.transpose(2, 0, 1).reshape(KC, P, 2, 104).transpose(1, 0, 2, 3), "cols": cols,
        "loc": np.tile(np.arange(S), B).astype(f)[None], "sel": sel, "zsel": zsel, "bsel": bsel,
        "ident": np.eye(P, dtype=f), "vld": vld, "wo": wo,
        "rows": np.stack([a["L0_xattn_bo"], a["L0_attn_b_C"], a["L0_attn_b_D"]]), "wb": kt(a["L0_attn_W_B"]),
        "wc": kt(a["L0_attn_W_C"]), "wd": kt(a["L0_attn_W_D"]), "rw": kt(a["L0_ffn_router_weight"]),
        "rb": a["L0_ffn_router_bias"][None], "low": np.concatenate([low4.ravel(), low16.ravel()])[None],
        "ltri": (p[:, None] < p[None, :]).astype(f), "iota": np.arange(T).astype(np.float16)[None],
        "tokc": np.concatenate([p[:, None] + P * np.arange(NT)[None] + 1, p[:, None] + T + 1], 1).astype(f),
        "wgu": wgu, "wdn": wdn,
    }


def kernel(**inputs):
    import concourse.bacc as _bacc
    from concourse import mybir as _mybir
    from concourse.bass_utils import run_bass_kernel_spmd as _run

    nc = _bacc.Bacc("TRN2", target_bir_lowering=False, num_devices=1)
    data = laid_out({k: np.asarray(v) for k, v in inputs.items()})
    arrays, io = {}, {}
    for name, shape, dt in INPUTS:
        a = np.ascontiguousarray(data[name])
        assert a.shape == shape, (name, a.shape)
        arrays[f"in_{name}"] = a
        io[name] = nc.dram_tensor(f"in_{name}", shape, dt, kind="ExternalInput").ap()
    out = nc.dram_tensor("out_0", (T + P, D), F32, kind="ExternalOutput").ap()
    program(nc, io, out)
    r = _run(nc, [arrays], core_ids=[0])
    return r.results[0]["out_0"][0:T].reshape(B, S, D)
```

```python
from contextlib import ExitStack

import numpy as np

import concourse.bass as bass
from concourse import mybir

P = 128
B, S, D, M = 8, 64, 512, 1601
T = B * S
NT = T // P
KC = D // P
H, NK = 16, 5
HD = D // H
NB = 13
DEAD = 32
E, I = 16, 256
EPS = 1e-5
MAGIC = 12582912.0

ALU = mybir.AluOpType
ACT = mybir.ActivationFunctionType
AX = mybir.AxisListType
F32 = mybir.dt.float32
F16 = mybir.dt.float16
I32 = mybir.dt.int32

C_BOFF, C_REF, C_BQ, C_BB, C_LOGA, C_DT, C_VLD, C_NEGP, C_N = 0, 2, 4, 8, 12, 16, 17, 18, 19

INPUTS = [
    ("x", (T, D), F32), ("ctx", (NB, P, B, KC, P), F32), ("mask", (P, B, 13), I32),
    ("wkv", (P, KC, 2 * D), F32), ("bkv", (1, 2 * D), F32), ("wq", (P, KC, D), F32),
    ("woff", (P, KC, 2, 104), F32), ("cols", (P, C_N), F32), ("loc", (1, T), F32),
    ("sel", (104, 40), F16), ("zsel", (P, 2, 126), F32), ("bsel", (P, 32, P), F16),
    ("ident", (P, P), F32), ("vld", (NB, P, 1), F32), ("wo", (P, 4, D), F32),
    ("rows", (3, D), F32), ("wb", (P, KC, D), F32), ("wc", (P, KC, D), F32),
    ("wd", (P, KC, D), F32), ("rw", (P, KC, E), F32), ("rb", (1, E), F32),
    ("low", (1, 16 + 256), F32), ("ltri", (P, P), F32), ("iota", (1, T), F16),
    ("tokc", (P, 5), F32), ("wgu", (E, P, KC, 2 * I), F32), ("wdn", (E, P, 2, D), F32),
]


class Queue:

    def __init__(self, sem):
        self.sem, self.n, self.at, self.items, self.last = sem, 0, {}, [], None

    def do(self, fn, mark=None, wait=()):
        if mark:
            self.n += 1
            self.at[mark] = self.n
            self.last = mark
        self.items.append((fn, mark, wait))


def emit(q, eng, queues, dsem):
    seen = {}
    for fn, mark, wait in q.items:
        for w in wait:
            who, what = w.split(".", 1)
            sem, value = (dsem[what], 16) if who == "d" else (queues[who].sem, queues[who].at[what])
            if seen.get((who, what) if who == "d" else who, 0) < value:
                seen[(who, what) if who == "d" else who] = value
                eng.wait_ge(sem, value)
        ins = fn()
        if mark:
            ins.then_inc(q.sem, 1)


def program(nc, io, out):
    with ExitStack() as ctx:
        def sb(name, shape, dt=F32):
            return ctx.enter_context(nc.sbuf_tensor(name, shape, dt))

        def sem(name):
            return ctx.enter_context(nc.semaphore(name))

        acc_r = sb("acc_r", [P, 20480])
        kv_r = sb("kv_r", [P, 8192])
        wkv_r = sb("wkv_r", [P, 4096])
        ctx_r = sb("ctx_r", [P, 4096])
        qm_r = sb("qm_r", [P, 4096])
        w_r = sb("w_r", [P, 5120])
        ix = sb("ix", [104, 2 * T])
        rp = sb("rp", [104, 2 * T], F16)
        bkv = sb("bkv", [P, 2 * D])
        sel = sb("sel", [104, 40], F16)
        cols = sb("cols", [P, C_N])
        ident = sb("ident", [P, P])
        mk = sb("mk", [P, B, 13], I32)
        ones = sb("ones", [P, P])
        zsel = sb("zsel", [P, 2, 126])
        st6 = sb("st6", [P, NT, 6])
        st2 = sb("st2", [P, NT, 2])
        rstd = sb("rstd", [P, NT])
        small = sb("small", [P, 64])
        flagi = sb("flagi", [1, 1], I32)
        vcol = sb("vcol", [P, 1])
        tmpg = sb("tmpg", [P, 320])
        rbt = sb("rbt", [P, E])
        lowt = sb("lowt", [P, 272])
        comb = sb("comb", [P, NT, E])
        tokc = sb("tokc", [P, 5])
        cnt = sb("cnt", [1, E], I32)
        slot_rows = sb("slot_rows", [P, (E - 1) * NT], I32)
        psum = ctx.enter_context(nc.psum_tensor("psum", [P, 8, 512], F32))

        def bank(i):
            return psum[:, i, :]

        acc = acc_r[:, :].rearrange("p (u c) -> p u c", c=320)
        kv = kv_r[:, :].rearrange("p (b e) -> p b e", b=B)
        wkv = wkv_r[:, :].rearrange("p (k e) -> p k e", k=KC)
        ctxt = ctx_r[:, :].rearrange("p (b k m) -> p b k m", b=B, k=KC)
        qm = qm_r[:, :].rearrange("p (t n) -> p t n", t=8)
        hat = w_r[:, :].rearrange("p (s r n) -> p s r n", s=2, r=10)

        def part(base, off, n):
            return base[:, off:off + n]

        def tile4(base, off):
            return part(base, off, 2048).rearrange("p (k n) -> p k n", k=4)

        xa, xna, xta, wq, qpt = (tile4(acc_r, 2048 * i) for i in range(5))
        woff = part(acc_r, 10240, KC * 208).rearrange("p (k g c) -> p k g c", k=KC, g=2)
        pos = [acc_r[0:104, 11264 + 1024 * i:12288 + 1024 * i] for i in range(4)]
        loct = acc_r[0:104, 15360:15872]

        bsel = kv_r[:, 0:2048].bitcast(F16).rearrange("p (u c) -> p u c", c=P)
        wo = kv_r[:, 2048:4096].rearrange("p (t n) -> p t n", t=4)
        ctxp = wkv_r[:, 0:2048].rearrange("p (t n) -> p t n", t=4)
        xr = tile4(ctx_r, 0)
        rowt = ctx_r[:, 2048:2048 + 3 * D].rearrange("p (r n) -> p r n", r=3)
        wb, wc = tile4(qm_r, 0), tile4(qm_r, 2048)
        wd = tile4(w_r, 2048)
        xn2, xt2, bu, coef, xs, xn3, xt3 = (tile4(acc_r, 2048 * i) for i in range(7))
        abar = small[:, 0:4]
        dtc = small[:, 4:5]
        rw = w_r[:, 0:KC * E].rearrange("p (k e) -> p k e", k=KC)
        xh = acc_r[:, 0:1024].bitcast(F16).rearrange("p (m d) -> p m d", m=NT)
        xl = acc_r[:, 1024:2048].bitcast(F16).rearrange("p (m d) -> p m d", m=NT)
        iota = acc_r[:, 2048:2304].bitcast(F16)
        picks = [acc_r[:, 2304 + 256 * i:2560 + 256 * i].bitcast(F16).rearrange("p (m s) -> p m s", m=NT)
                 for i in range(4)]
        xg = acc_r[:, 3328:3840]
        ltri = acc_r[:, 3840:3968]
        silu0 = acc_r[:, 8192:9216]
        hid0 = acc_r[:, 9216:10240].rearrange("p (i n) -> p i n", i=2)
        ys = [acc_r[:, 8192 + 512 * i:8704 + 512 * i] for i in range(10)]
        silu = w_r[:, 512:768]
        hid = w_r[:, 768:1024]
        hidt = w_r[:, 1024:1280]
        rh = w_r[:, 1280:1408].bitcast(F16).rearrange("p (m e c) -> p m e c", m=NT, e=E)
        posm = w_r[:, 1408:1472]
        selc = w_r[:, 1472:1552].rearrange("p (m e) -> p m e", m=5)
        lst = w_r[:, 1552:1556]
        pad = w_r[:, 1556:1557]
        wcol = w_r[:, 1557:1558]
        NW = 6
        wbufs = [kv_r[:, 0:3072], kv_r[:, 3072:6144], acc_r[:, 14336:17408], acc_r[:, 17408:20480],
                 wkv_r[:, 0:3072], qm_r[:, 0:3072]]
        rt = [acc_r[:, 4096 + 1024 * i:5120 + 1024 * i] for i in range(4)]

        Q = {k: Queue(sem("s_" + k)) for k in "vapsg"}
        V, A, PE, SP, GP = Q["v"], Q["a"], Q["p"], Q["s"], Q["g"]
        dsem = {}
        ve, ae, pe, sp, gp = nc.vector, nc.scalar, nc.tensor, nc.sync, nc.gpsimd
        s_out = sem("s_out")

        def load(name, dst, src, wait=()):
            dsem[name] = sem("d_" + name)
            SP.do(lambda: sp.dma_start(dst, src).then_inc(dsem[name], 16), wait=wait)

        auto = [0]

        def v(fn, mark=None, wait=()):
            if mark is None:
                auto[0] += 1
                mark = f"auto{auto[0]}"
            own = ("v." + V.last,) if V.last else ()
            V.do(fn, mark, own + tuple(wait))

        def vi(fn, mark, wait=()):
            V.do(fn, mark, wait)

        for m in range(NT):
            load(f"xin{m}", xa[:, m, :], io["x"].rearrange("(m p) d -> p m d", p=P)[:, m, :])
        load("cols", cols[:, :], io["cols"])
        load("ident", ident[:, :], io["ident"])
        load("wq", wq, io["wq"])
        load("woff", woff, io["woff"])
        load("mask", mk[:, :, :], io["mask"])
        load("sel", sel[:, :], io["sel"])
        load("loc", loct, io["loc"].broadcast_to([104, T]))
        load("ctx0", ctxt, io["ctx"][0])
        load("wkv", wkv, io["wkv"])
        load("bkv", bkv[:, :], io["bkv"].broadcast_to([P, 2 * D]))
        load("zsel", zsel[:, :, :], io["zsel"])
        load("rb", rbt[:, :], io["rb"].broadcast_to([P, E]))
        load("low", lowt[:, :], io["low"].broadcast_to([P, 272]))
        load("tokc", tokc[:, :], io["tokc"])

        def stats(tag, src, m, wait):
            vi(lambda: ve.bn_stats(st6[:, m, :], src[:, m, :]), f"{tag}.st{m}", wait)

        def variance(tag, m):
            vi(lambda: ve.bn_aggr(st2[:, m, :], st6[:, m, :]), f"{tag}.ag{m}", (f"v.{tag}.st{m}",))
            A.do(lambda: ae.activation(rstd[:, m:m + 1], st2[:, m, 1:2], ACT.Sqrt, bias=small[:, 60:61]),
                 f"{tag}.sd{m}", (f"v.{tag}.ag{m}", "v.eps"))

        def inverse(tag, m):
            r = rstd[:, m:m + 1]
            vi(lambda: ve.reciprocal(r, r), f"{tag}.rs{m}", (f"a.{tag}.sd{m}",))

        def scaled(tag, src, dst, m):
            r = rstd[:, m:m + 1]
            vi(lambda: ve.tensor_scalar(dst[:, m, :], src[:, m, :], st2[:, m, 0:1], r, ALU.subtract, ALU.mult),
               f"{tag}.xn{m}", (f"v.{tag}.rs{m}",))

        def normalise(tag, src, dst, m):
            inverse(tag, m)
            scaled(tag, src, dst, m)

        def transposes(tag, src, base, m, wait=()):
            for k in range(KC):
                PE.do(lambda k=k: pe.transpose(psum[:, base + k, m * P:(m + 1) * P],
                                               src[:, m, k * P:(k + 1) * P], ident[:, :]),
                      f"{tag}.t{k}" if m == NT - 1 else None, (f"v.{tag}.xn{m}", "d.ident") + tuple(wait))

        def by_chunk(tag):
            return lambda k: f"{'va'[k % 2]}.{tag}.xt{k}"

        def transposed(tag, dst, base):
            for k in range(KC):
                if k % 2:
                    A.do(lambda k=k: ae.activation(dst[:, k, :], bank(base + k), ACT.Copy), f"{tag}.xt{k}",
                         (f"p.{tag}.t{k}",))
                else:
                    vi(lambda k=k: ve.tensor_copy(dst[:, k, :], bank(base + k)), f"{tag}.xt{k}", (f"p.{tag}.t{k}",))

        def product(banks, lhs, rhs, n, mark, wait=(), rows=P, cols_=D, each=None):
            for k in range(n):
                PE.do(lambda k=k: pe.matmul(banks[0:rows, 0:cols_], lhs(k), rhs(k), start=(k == 0), stop=(k == n - 1)),
                      mark if k == n - 1 else None, (wait if k == 0 else ()) + ((each(k),) if each else ()))

        vi(lambda: ve.memset(small[:, 60:61], EPS), "eps")
        vi(lambda: ve.memset(ones[:, :], 1.0), "ones")
        for m in range(NT):
            stats("l1", xa, m, (f"d.xin{m}",))
            variance("l1", m)
            if m:
                normalise("l1", xa, xna, m - 1)
                transposes("l1", xna, 0, m - 1)
        normalise("l1", xa, xna, NT - 1)
        transposes("l1", xna, 0, NT - 1)
        transposed("l1", xta, 0)
        vi(lambda: ve.memset(qm_r[:, :], 1.0), "qm1")

        for m in range(4):
            product(bank(4 + m), lambda k, m=m: wq[:, k, m * P:(m + 1) * P], lambda k: xta[:, k, :], KC, f"q{m}",
                    ("d.wq",), each=by_chunk("l1"))
            vi(lambda m=m: ve.tensor_scalar(qpt[:, m, :], bank(4 + m), cols[:, C_BQ + m:C_BQ + m + 1], None, ALU.add),
               f"q{m}", (f"p.q{m}", "d.cols"))
        for h in range(H):
            m, i = h // 4, h % 4
            lo = 64 * (h % 2) + 32 * (h // 2 % 2)
            A.do(lambda m=m, i=i, lo=lo, h=h: ae.activation(qm[lo:lo + 32, h // 2, :], qpt[32 * i:32 * i + 32, m, :],
                                                            ACT.Copy),
                 f"qm{h}", (f"v.q{m}", "v.qm1"))

        for g in range(2):
            product(bank(g), lambda k, g=g: woff[:, k, g, :], lambda k: qpt[:, k, :], KC, f"off{g}",
                    ("d.woff", "v.l1.xt2"), rows=104, each=lambda k: f"v.q{k}")
        vi(lambda: ve.tensor_reduce(small[:, 8:16], mk[:, :, :], AX.X, ALU.add), "msum", ("d.mask",))
        PE.do(lambda: pe.matmul(psum[:, 2, 0:B], ones[:, :], small[:, 8:16], start=True, stop=True), "msum",
              ("v.msum", "v.ones", "v.l1.xt2"))

        def kv_proj(j):
            b, half = j // 2, j % 2
            product(bank(4 + j % 4), lambda k: ctxt[:, b, k, :], lambda k: wkv[:, k, half * D:(half + 1) * D], KC,
                    f"kv{j}", ("d.ctx0", "d.wkv", f"v.q{j}" if j < 4 else f"v.kv{j - 4}"))

        def kv_evac(j):
            b, half = j // 2, j % 2
            vi(lambda: ve.scalar_tensor_tensor(out=kv[:, b, half * D:(half + 1) * D],
                                               in0=bkv[:, half * D:(half + 1) * D], scalar=cols[:, C_VLD:C_VLD + 1],
                                               in1=bank(4 + j % 4), op0=ALU.mult, op1=ALU.add),
               f"kv{j}", (f"p.kv{j}", "d.bkv", "d.cols"))

        for j in range(14):
            if j == 11:
                PE.do(lambda: pe.transpose(psum[0:1, 3, 0:104], small[0:104, 32:33], ident[0:104, 0:104]), "far",
                      ("v.pos.far",))
            kv_proj(j)

        t0, t1, t2, lf = pos
        c104 = cols[0:104, :]
        steps = []

        def pstep(fn, mark=None, wait=()):
            steps.append((fn, mark, wait))

        msb = small[0:104, 16:24]
        inv = small[0:104, 24:32]

        def by_batch(ap):
            return ap.unsqueeze(1).unsqueeze(3).broadcast_to([104, 2, B, S])

        def four(ap):
            return ap.rearrange("p (g b q) -> p g b q", g=2, b=B)

        pstep(lambda: ve.tensor_scalar(msb, psum[0:104, 2, 0:B], -1.0, float(M - 1), ALU.mult, ALU.add), "len",
              ("p.msum",))
        pstep(lambda: ve.reciprocal(inv, msb))
        pstep(lambda: ve.tensor_copy(four(lf), by_batch(msb)))
        for g in range(2):
            pstep(lambda g=g: ve.tensor_scalar(t0[:, g * T:(g + 1) * T], psum[0:104, g, :],
                                               c104[:, C_BOFF + g:C_BOFF + g + 1], c104[:, C_REF + g:C_REF + g + 1],
                                               ALU.add, ALU.add), f"off{g}", (f"p.off{g}",))
        pstep(lambda: ve.tensor_tensor(t0.rearrange("p (g n) -> p g n", g=2), t0.rearrange("p (g n) -> p g n", g=2),
                                       loct.unsqueeze(1).broadcast_to([104, 2, T]), ALU.add), "loc", ("d.loc",))
        pstep(lambda: ve.tensor_tensor(four(t1), four(t0), by_batch(inv), ALU.mult))
        pstep(lambda: ve.tensor_scalar(t1, t1, MAGIC, MAGIC, ALU.add, ALU.subtract))
        pstep(lambda: ve.tensor_tensor(t1, t1, lf, ALU.mult))
        pstep(lambda: ve.tensor_tensor(t0, t0, t1, ALU.subtract))
        pstep(lambda: ve.tensor_tensor(t1, t0, lf, ALU.mult))
        pstep(lambda: ve.scalar_tensor_tensor(out=t1, in0=t1, scalar=0.0, in1=lf, op0=ALU.is_lt, op1=ALU.mult))
        pstep(lambda: ve.tensor_tensor(t0, t0, t1, ALU.add))
        pstep(lambda: ve.tensor_scalar(t0, t0, 1.0 / (M - 1), 2.0, ALU.mult, ALU.mult))
        pstep(lambda: ve.tensor_scalar(t0, t0, -1.0, 1.0, ALU.add, ALU.add))
        pstep(lambda: ve.tensor_scalar(t0, t0, float(M), -1.0, ALU.mult, ALU.add))
        pstep(lambda: ve.tensor_scalar(ix[:, :], t0, 0.5, None, ALU.mult))
        pstep(lambda: ve.tensor_scalar(t1, ix[:, :], 800.0, float(M + 1), ALU.is_ge, ALU.mult))
        pstep(lambda: ve.tensor_tensor(t0, ix[:, :], t1, ALU.subtract))
        pstep(lambda: ve.tensor_scalar(t0, t0, float(DEAD + 1 - 64), None, ALU.add))
        pstep(lambda: ve.tensor_scalar(t1, t0, 0.5, None, ALU.add))
        pstep(lambda: ve.tensor_reduce(small[0:104, 32:33], t1, AX.X, ALU.max, apply_absolute_value=True), "far")
        pstep(lambda: ve.tensor_scalar(t1, t0, 66.0, -66.0, ALU.min, ALU.max))
        pstep(lambda: ve.tensor_copy(rp[:, :], t1))
        pstep(lambda: ve.tensor_tensor(rp[64:104, :], t1[64:104, :], rp[64:104, :], ALU.subtract), "rp")

        def flag():
            v(lambda: ve.tensor_reduce(small[0:1, 33:34], psum[0:1, 3, 0:104], AX.X, ALU.max), None, ("p.far",))
            v(lambda: ve.tensor_scalar(flagi[0:1, :], small[0:1, 33:34], 63.5, None, ALU.is_gt), "flag")

        evacs = list(range(14))
        pos_at = 0
        while steps or evacs:
            for _ in range(3):
                if steps:
                    fn, mark, wait = steps.pop(0)
                    v(fn, mark and "pos." + mark, tuple(wait) + ("d.cols",))
            if evacs and pos_at >= 1 or not steps:
                if evacs:
                    kv_evac(evacs.pop(0))
                    if evacs and evacs[0] == 11:
                        flag()
            pos_at += 1

        units = [(t, half) for t in range(8) for half in range(2)]
        chunks = [(0, 4), (4, 8), (8, 10)]

        def head_row(t, r):
            h = 2 * t + r // 5
            return h // 8, (h % 8) * 5 + r % 5

        def spread(t, half, c, slot):
            out_ = []
            for i, r in enumerate(range(*chunks[c])):
                g, row = head_row(t, r)
                out_.append(lambda i=i, g=g, row=row: pe.matmul(
                    psum[:, 2 * slot + i // 2, (i % 2) * 256:(i % 2) * 256 + 256],
                    sel[:, row:row + 1].broadcast_to([104, P]),
                    rp[:, g * T + half * 256:g * T + half * 256 + 256], start=True, stop=True))
            return out_

        def hat_abs(s, c, slot):
            r0, r1 = chunks[c]
            n = (r1 - r0) * 256
            src = psum[:, 2 * slot:2 * slot + 2, :].rearrange("p a n -> p (a n)")[:, 0:n]
            return ae.activation(hat[:, s, r0:r1, :].rearrange("p r n -> p (r n)"), src, ACT.Abs,
                                 bias=cols[:, C_NEGP:C_NEGP + 1])

        def hat_low(s, c):
            w = hat[:, s, chunks[c][0]:chunks[c][1], :]
            return ve.tensor_scalar(w, w, 1.0, 1.0, ALU.min, ALU.subtract)

        def sampled(t, half, bb, s, g):
            b = 4 * half + bb
            out_ = []
            for i in range(2):
                h = 2 * t + i
                out_.append(lambda i=i, h=h: pe.matmul(
                    psum[64 * i:64 * i + 64, g, 0:320], kv[:, b, h * 64:(h + 1) * 64],
                    hat[:, s, 5 * i:5 * i + 5, bb * S:(bb + 1) * S], start=True, stop=True))
            return out_

        def weighed(out_, t, b, g):
            return ve.tensor_tensor(out_.rearrange("p (k q) -> p k q", k=NK),
                                    psum[:, g, 0:320].rearrange("p (k q) -> p k q", k=NK),
                                    qm[:, t, b * S:(b + 1) * S].unsqueeze(1).broadcast_to([P, NK, S]), ALU.mult)

        def pe_spread(n, c):
            t, half = units[n]
            x = 3 * n + c
            fns = spread(t, half, c, x % 2)
            w = ("v.pos.rp", "d.sel", "v.flag") + ((f"a.hat{x - 2}",) if x >= 2 else ("a.l1.xt3", "v.l1.xt2"))
            for i, fn in enumerate(fns):
                PE.do(fn, f"sp{x}" if i == len(fns) - 1 else None, w)

        def pe_sample(n, bbs):
            t, half = units[n]
            for bb in bbs:
                y = 4 * n + bb
                w = (f"v.low{3 * n + 2}", "v.kv15") + ((f"v.g{y - 4}",) if y >= 4 else ())
                fns = sampled(t, half, bb, n % 2, 4 + y % 4)
                for i, fn in enumerate(fns):
                    PE.do(fn, f"g{y}" if i == 1 else None, w)

        far = {}

        def load_flag(q, eng):
            def run():
                far[eng] = eng.value_load(flagi[0:1, 0:1], min_val=0, max_val=1)
            q.do(run, None, ("v.flag",))

        NU = len(units)
        for n in range(NU + 1):
            if n < NU:
                for c in range(3):
                    if c == 2 and n:
                        pe_sample(n - 1, (0, 1))
                    if c == 2 and not n:
                        for j in (14, 15):
                            kv_proj(j)
                            kv_evac(j)
                        for q, eng in ((V, ve), (A, ae), (PE, pe), (SP, sp)):
                            load_flag(q, eng)
                    pe_spread(n, c)
                    x = 3 * n + c
                    A.do(lambda n=n, c=c, x=x: hat_abs(n % 2, c, x % 2), f"hat{x}",
                         (f"p.sp{x}",) + ((f"p.g{4 * (n - 2) + 3}",) if n >= 2 else ("v.flag",)))
                    vi(lambda n=n, c=c: hat_low(n % 2, c), f"low{x}", (f"a.hat{x}",))
            if n >= 1:
                pe_sample(n - 1, (2, 3) if n < NU else range(4))
                t, half = units[n - 1]
                for bb in range(4):
                    y = 4 * (n - 1) + bb
                    b = 4 * half + bb
                    vi(lambda t=t, b=b, y=y: weighed(acc[:, t * 8 + b, :], t, b, 4 + y % 4), f"g{y}",
                       (f"p.g{y}", "a.qm15"))

        g_d, g_kvp, g_kvv, g_rp, g_sp, g_hat, g_low, g_gp, g_gv, g_arr = (
            sem("g_" + n) for n in ("d", "kvp", "kvv", "rp", "sp", "hat", "low", "gp", "gv", "arr"))
        g_go = {e: sem("g_go" + e) for e in "vap"}
        g_all = [g_d, g_kvp, g_kvv, g_rp, g_sp, g_hat, g_low, g_gp, g_gv, g_arr]
        g_ini = sem("g_ini")

        def rest(eng, who, body, first=None, last=None):
            def run():
                with eng.If(far[eng]):
                    if first:
                        first()
                    with eng.Fori(1, NB) as j:
                        body(j)
                        if who != "s":
                            eng.sem_inc(g_arr, 1)
                            eng.wait_ge(g_go[who], 1)
                            eng.sem_clear(g_go[who])
                        else:
                            eng.wait_ge(g_arr, 3)
                            for s in g_all:
                                eng.sem_clear(s)
                            for s in g_go.values():
                                eng.sem_inc(s, 1)
            return run

        def rest_sp(j):
            sp.dma_start(ctx_r[:, :], io["ctx"].rearrange("j p b k m -> j p (b k m)")[bass.DynSlice(j, 1), :, :]
                         .rearrange("a p n -> (a p) n")).then_inc(g_d, 16)
            sp.dma_start(vcol[:, :], io["vld"][bass.DynSlice(j, 1), :, :].rearrange("a p n -> (a p) n")).then_inc(g_d, 16)
            sp.wait_ge(g_d, 32)

        def rest_v(j):
            ve.tensor_scalar(t1g, ix[:, :], 66.0, -66.0, ALU.min, ALU.max).then_inc(g_rp, 1)
            ve.wait_ge(g_rp, 1)
            ve.tensor_copy(rp[:, :], t1g).then_inc(g_rp, 1)
            ve.wait_ge(g_rp, 2)
            ve.tensor_tensor(rp[64:104, :], t1g[64:104, :], rp[64:104, :], ALU.subtract).then_inc(g_rp, 1)
            ve.wait_ge(g_rp, 3)
            ve.tensor_scalar(ix[:, :], ix[:, :], -128.0, None, ALU.add).then_inc(g_rp, 1)
            ve.wait_ge(g_rp, 4)
            ve.wait_ge(g_d, 32)
            for j2 in range(16):
                b, half = j2 // 2, j2 % 2
                ve.wait_ge(g_kvp, j2 + 1)
                ve.scalar_tensor_tensor(out=kv[:, b, half * D:(half + 1) * D], in0=bkv[:, half * D:(half + 1) * D],
                                        scalar=vcol[:, 0:1], in1=bank(4 + j2 % 4), op0=ALU.mult,
                                        op1=ALU.add).then_inc(g_kvv, 1)
            for n in range(NU):
                t, half = units[n]
                for c in range(3):
                    ve.wait_ge(g_hat, 3 * n + c + 1)
                    hat_low(0, c).then_inc(g_low, 1)
                for bb in range(4):
                    y = 4 * n + bb
                    b = 4 * half + bb
                    ve.wait_ge(g_gp, y + 1)
                    weighed(tmpg[:, :], t, b, 4 + y % 4).then_inc(g_gv, 1)
                    ve.wait_ge(g_gv, 2 * y + 1)
                    ve.tensor_tensor(acc[:, t * 8 + b, :], acc[:, t * 8 + b, :], tmpg[:, :], ALU.add).then_inc(g_gv, 1)
                    ve.wait_ge(g_gv, 2 * y + 2)

        t1g = w_r[0:104, 2560:3584]

        def rest_v_first():
            ve.tensor_scalar(ix[:, :], ix[:, :], float(DEAD + 1 - P - 64), None, ALU.add).then_inc(g_ini, 1)
            ve.wait_ge(g_ini, 1)

        def rest_a(j):
            for n in range(NU):
                for c in range(3):
                    x = 3 * n + c
                    ae.wait_ge(g_sp, x + 1)
                    if n >= 1:
                        ae.wait_ge(g_gp, 4 * n)
                    hat_abs(0, c, x % 2).then_inc(g_hat, 1)

        def rest_p(j):
            pe.wait_ge(g_d, 32)
            for j2 in range(16):
                b, half = j2 // 2, j2 % 2
                if j2 >= 4:
                    pe.wait_ge(g_kvv, j2 - 3)
                for k in range(KC):
                    mm = pe.matmul(bank(4 + j2 % 4), ctxt[:, b, k, :], wkv[:, k, half * D:(half + 1) * D],
                                   start=(k == 0), stop=(k == KC - 1))
                mm.then_inc(g_kvp, 1)
            pe.wait_ge(g_rp, 3)
            pe.wait_ge(g_kvv, 16)
            for n in range(NU):
                t, half = units[n]
                for c in range(3):
                    x = 3 * n + c
                    if x >= 2:
                        pe.wait_ge(g_hat, x - 1)
                    for fn in spread(t, half, c, x % 2):
                        mm = fn()
                    mm.then_inc(g_sp, 1)
                pe.wait_ge(g_low, 3 * n + 3)
                for bb in range(4):
                    y = 4 * n + bb
                    if y >= 4:
                        pe.wait_ge(g_gv, 2 * (y - 3))
                    for fn in sampled(t, half, bb, 0, 4 + y % 4):
                        mm = fn()
                    mm.then_inc(g_gp, 1)

        first_done = ("v.g63", "p.g63", "v.flag")
        SP.do(rest(sp, "s", rest_sp), wait=first_done)
        V.do(rest(ve, "v", rest_v, first=rest_v_first), wait=first_done)
        A.do(rest(ae, "a", rest_a), wait=first_done)
        PE.do(rest(pe, "p", rest_p), wait=first_done)
        vi(lambda: ve.memset(small[0:1, 40:41], 0.0), "rest")

        free = ("v.rest",)
        load("bsel", bsel, io["bsel"], free)
        load("wo", wo, io["wo"], free)
        load("x2", xr, io["x"].rearrange("(m p) d -> p m d", p=P), free)
        load("rows", rowt, io["rows"].unsqueeze(0).broadcast_to([P, 3, D]), free)
        load("wb", wb, io["wb"], free)
        load("wc", wc, io["wc"], free)
        load("wd", wd, io["wd"], free)

        def add_row(r, dst, wait):
            vi(lambda: ve.tensor_tensor(dst, dst, rowt[:, r, :].unsqueeze(1).broadcast_to([P, NT, D]), ALU.add),
               f"row{r}", wait)

        def scores(w0, w1):
            for w in range(w0, w1):
                for o in range(2):
                    PE.do(lambda w=w, o=o: pe.matmul(psum[64 * o:64 * o + 64, w // 16, 0:320],
                                                     zsel[:, o, 62 - 2 * w:126 - 2 * w],
                                                     acc[:, 16 * (w // 8) + w % 8 + 8 * o, :],
                                                     start=(w % 16 == 0), stop=(w % 16 == 15)),
                          f"score{w // 8}" if w % 8 == 7 and o else None, ("v.rest", "d.zsel", "a.hat47"))

        def join(j):
            for base, q, who in ((0, A, ae), (64, V, ve)):
                def run(base=base, who=who):
                    dst = acc_r[base:base + 32, 5120 * j:5120 * j + 2560]
                    src = acc_r[base:base + 32, 5120 * j + 2560:5120 * j + 5120]
                    return who.tensor_copy(dst, src) if who is ve else who.activation(dst, src, ACT.Copy)
                q.do(run, f"join{j}", (f"p.score{j}",))

        def kq(ap):
            return ap.rearrange("p (k q) -> p k q", k=NK)

        def qk(ap):
            return ap.rearrange("p (k q) -> p q k", k=NK)

        def over_k(ap):
            return ap.unsqueeze(1).broadcast_to([P, NK, S])

        def softmax(g):
            o = 1024 * g
            sc, ex, mn, sm, rc = (w_r[:, o + a:o + b] for a, b in ((0, 320), (320, 640), (640, 704), (704, 768),
                                                                   (768, 832)))
            hi, lo = w_r[:, o + 832:o + 992].bitcast(F16), sc[:, 0:160].bitcast(F16)
            raw = psum[:, g, 0:320]
            return [
                lambda: vi(lambda: ve.tensor_reduce(mn, qk(raw), AX.X, ALU.min), f"mn{g}", (f"p.score{2 * g + 1}",)),
                lambda: vi(lambda: ve.tensor_tensor(kq(sc), kq(raw), over_k(mn), ALU.subtract), f"sc{g}",
                           (f"v.mn{g}",)),
                lambda: A.do(lambda: ae.activation(ex, sc, ACT.Exp, scale=-0.5 / HD ** 0.5), f"ex{g}",
                             (f"v.sc{g}",)),
                lambda: vi(lambda: ve.tensor_reduce(sm, qk(ex), AX.X, ALU.add), f"sm{g}", (f"a.ex{g}",)),
                lambda: vi(lambda: ve.reciprocal(rc, sm), f"rc{g}", (f"v.sm{g}",)),
                lambda: vi(lambda: ve.tensor_scalar(rc, rc, -0.5, None, ALU.mult), f"rh{g}", (f"v.rc{g}",)),
                lambda: vi(lambda: ve.tensor_tensor(kq(ex), kq(ex), over_k(rc), ALU.mult), f"exn{g}",
                           (f"v.rh{g}",)),
                lambda: vi(lambda: ve.tensor_copy(hi, ex), f"ahi{g}", (f"v.exn{g}",)),
                lambda: vi(lambda: ve.tensor_tensor(lo, ex, hi, ALU.subtract), f"at{g}", (f"v.ahi{g}",)),
            ], (hi, lo)

        def av(w, halves):
            g, u = w // 16, 16 * (w // 8) + w % 8
            for i, a in enumerate(halves):
                PE.do(lambda i=i, a=a: pe.matmul(psum[:, 4 + w % 4, 0:320], bsel[:, w, :], a, start=(i == 0),
                                                 stop=(i == 1)), f"av{w}" if i else None,
                      (f"v.at{g}", "d.bsel") + ((f"v.av{w - 4}",) if w >= 4 else ()))
            vi(lambda: ve.tensor_tensor(acc[:, u, :], acc[:, u, :], psum[:, 4 + w % 4, 0:320], ALU.mult),
               f"av{w}", (f"p.av{w}", f"a.join{w // 8}", f"v.join{w // 8}"))
            if w % 4 == 3:
                dst = wkv_r[:, (w - 3) * S:(w + 1) * S].rearrange("p (u q) -> p u q", u=4)
                part_ = [acc[:, u - 3:u + 1, k * S:(k + 1) * S] for k in range(NK)]
                if w in POOL:
                    for k in range(1, NK):
                        a = part_[0] if k == 1 else dst
                        GP.do(lambda a=a, k=k: gp.tensor_tensor(dst, a, part_[k], ALU.add), f"ctx{w}.{k}",
                              (f"v.av{w}",) + ((f"g.{GP.last}",) if GP.last else ()))
                else:
                    v(lambda: ve.tensor_reduce(dst, acc[:, u - 3:u + 1, :].rearrange("p u (k q) -> p u q k", k=NK),
                                               AX.X, ALU.add), f"ctx{w}")

        LAG, EARLY, GAPS = 13, 4, (1, 2, 3, 4, 5, 6, 7)
        POOL = (3, 7, 11, 19, 23)
        GP.do(lambda: gp.tensor_tensor(xr, xr, rowt[:, 0, :].unsqueeze(1).broadcast_to([P, NT, D]), ALU.add), "row0",
              ("d.x2", "d.rows"))
        scores(0, 28)
        join(0)
        join(1)
        steps0, half0 = softmax(0)
        steps1, half1 = softmax(1)
        halves = [half0, half1]
        for step in steps0:
            step()
        join(2)
        for w in range(EARLY):
            av(w, halves[0])
        scores(28, 32)
        w = EARLY
        for i, step in enumerate(steps1):
            step()
            if i in GAPS:
                av(w, halves[0])
                w += 1
        join(3)

        def out_part(j):
            k, m = j // NT, j % NT
            PE.do(lambda: pe.matmul(bank(m), ctxp[:, k, m * P:(m + 1) * P], wo[:, k, :], start=(k == 0),
                                    stop=(k == 3)), f"o{m}" if k == 3 else None,
                  ("v.at1", "d.wo") + tuple(f"g.ctx{w}.4" if w in POOL else f"v.ctx{w}"
                                            for w in (8 * k + 3, 8 * k + 7)))

        parts = list(range(16))
        for w in range(w, 32):
            av(w, halves[w // 16])
            while w >= LAG and w % 2 and parts and 2 * (16 - len(parts)) + LAG <= w:
                out_part(parts.pop(0))
        for j in parts:
            out_part(j)

        A.do(lambda: ae.activation(dtc, cols[:, C_DT:C_DT + 1], ACT.Exp), "dt", ("d.cols",))
        A.do(lambda: ae.activation(abar, cols[:, C_LOGA:C_LOGA + 4], ACT.Exp), "ea", ("v.rest",))
        v(lambda: ve.tensor_scalar(abar, abar, dtc, -1.0, ALU.mult, ALU.mult), "adt", ("a.dt", "a.ea"))
        A.do(lambda: ae.activation(abar, abar, ACT.Exp), "abar", ("v.adt",))
        for m in range(NT):
            vi(lambda m=m: ve.tensor_tensor(xr[:, m, :], xr[:, m, :], bank(m), ALU.add), f"x1.{m}",
               (f"p.o{m}", "g.row0"))
            if m:
                inverse("l2", m - 1)
            stats("l2", xr, m, (f"v.x1.{m}",))
            if m:
                scaled("l2", xr, xn2, m - 1)
            variance("l2", m)
            if m:
                transposes("l2", xn2, 4, m - 1, ("v.av31",))
        normalise("l2", xr, xn2, NT - 1)
        transposes("l2", xn2, 4, NT - 1)
        transposed("l2", xt2, 4)

        for k in range(KC):
            v(lambda k=k: ve.tensor_copy(coef[:, k, :], abar[:, k:k + 1].broadcast_to([P, T])), None, ("a.abar",))
        v(lambda: ve.memset(coef.rearrange("p k (b t) -> p k b t", b=B)[:, :, :, 0:1], 0.0), "coef")
        for m in range(4):
            product(bank(m), lambda k, m=m: wb[:, k, m * P:(m + 1) * P], lambda k: xt2[:, k, :], KC, f"bu{m}",
                    ("d.wb", "v.x1.3"), each=by_chunk("l2"))
            v(lambda m=m: ve.tensor_scalar(bu[:, m, :], bank(m), cols[:, C_BB + m:C_BB + m + 1], dtc, ALU.add,
                                           ALU.mult), f"bu{m}", (f"p.bu{m}",))
            v(lambda m=m: ve.tensor_tensor_scan(xs[:, m, :], coef[:, m, :], bu[:, m, :], 0.0, ALU.mult, ALU.add),
              f"xs{m}")
        add_row(1, xr, ("v.l2.xn3",))
        add_row(2, xr, ("v.row1",))
        for m in range(NT):
            for i in range(2 * KC):
                lhs, w, k = (xt2, wd, i) if i < KC else (xs, wc, i - KC)
                PE.do(lambda m=m, i=i, lhs=lhs, w=w, k=k: pe.matmul(
                    bank(4 + m), lhs[:, k, m * P:(m + 1) * P], w[:, k, :], start=(i == 0), stop=(i == 7)),
                    f"y{m}" if i == 7 else None, ("d.wd", "d.wc") if i < KC else (f"v.xs{k}",))
            v(lambda m=m: ve.tensor_tensor(xr[:, m, :], xr[:, m, :], bank(4 + m), ALU.add), f"x2.{m}", (f"p.y{m}",))
            stats("l3", xr, m, (f"v.x2.{m}",))
            variance("l3", m)
            normalise("l3", xr, xn3, m)
            if m:
                transposes("l3", xn3, 0, m - 1, ("v.bu3",))
        transposes("l3", xn3, 0, NT - 1)
        transposed("l3", xt3, 0)

        NE, HALF = E - 1, 64
        (p_lo, p_hi, p_list, p_turn, p_gate, p_down, v_first, v_pick, v_list, v_pad, v_rows, v_xg, v_hid, a_xg, a_silu,
         a_turn, a_y, g_dma, g_sum, g_turn, g_end) = (sem("t_" + n) for n in (
             "pl", "ph", "ps", "pt", "pg", "pd", "vf", "vp", "vl", "va", "vr", "vx", "vh", "ax", "as", "at", "ay",
             "gd", "gs", "gt", "ge"))
        counts, now, this, base1, base2, base3, base4, now16 = ({} for _ in range(8))

        def prepare(eng, name, own=()):
            def run():
                regs = [eng.alloc_register(f"{name}_cnt{n}") for n in range(NE)]
                eng.reg_load(regs, cnt[0:1, 1:E])
                counts[eng] = [eng.snap(r, donate=True, min_val=0, max_val=T) for r in regs]
                for what, regs, value in (
                        ("now", now, 1), ("this", this, 2), ("b1", base1, 1), ("b2", base2, 1), ("b3", base3, 1),
                        ("b4", base4, 1), ("n16", now16, 16)):
                    regs[eng] = eng.alloc_register(f"{name}_{what}")
                    eng.reg_mov(regs[eng], value)
                for s in own:
                    eng.sem_inc(s, 1)
            return run

        def pick(dst, n, i):
            for m in range(NT):
                c = m * E + n + 1
                op = ve.tensor_scalar(dst[:, m, :], iota[:, i * P:(i + 1) * P], posm[:, c:c + 1], None, ALU.is_equal)
            return op

        load("rw", rw, io["rw"], ("v.at1", "v.ctx31", "p.av31"))

        load("ltri", ltri, io["ltri"], ("p.y3",))
        load("iota", iota, io["iota"].broadcast_to([P, T]), ("p.y3",))
        for e in range(NW):
            w = wbufs[e % NW]
            wait = ("p.o3", "p.av31") if e < 2 else ("v.ctx31",) if e < 4 else ("p.o3",) if e == 4 else ("p.y3",)
            load(f"wgu{e}", w[:, 0:2048].rearrange("p (k n) -> p k n", k=KC), io["wgu"][e], wait)
            load(f"wdn{e}", w[:, 2048:3072].rearrange("p (i n) -> p i n", i=2), io["wdn"][e], wait)
        for m in range(NT):
            for k in range(KC):
                PE.do(lambda m=m, k=k: pe.matmul(psum[:, 4, m * E:(m + 1) * E], xt3[:, k, m * P:(m + 1) * P],
                                                 rw[:, k, :], start=(k == 0), stop=(k == 3)),
                      "route" if m == 3 and k == 3 else None, (by_chunk("l3")(k), "d.rw", "v.x2.3"))
        s0, s1, s2, s3 = rt
        scr = s0[:, 0:64]
        cho = s0[:, 64:128]
        prs = s0[:, 128:144 + 80]
        grp = s0[:, 256:272]
        gsel = s0[:, 272:288]
        mch = s0[:, 320:384]
        msel = s0[:, 384:448]
        wsum = s0[:, 448:452]
        A.do(lambda: ae.activation(scr, psum[:, 4, 0:64], ACT.Sigmoid), "scr", ("p.route", "v.xs3"))
        v(lambda: ve.tensor_tensor(cho.rearrange("p (m e) -> p m e", m=NT), scr.rearrange("p (m e) -> p m e", m=NT),
                                   rbt[:, :].unsqueeze(1).broadcast_to([P, NT, E]), ALU.add), None,
          ("a.scr", "d.rb", "p.y3"))
        c4 = cho.rearrange("p (g i) -> p g i", i=4)
        pr = s0[:, 128:224].rearrange("p (g j) -> p g j", j=6)
        v(lambda: ve.tensor_tensor(pr[:, :, 0:3], c4[:, :, 0:1].broadcast_to([P, 16, 3]), c4[:, :, 1:4], ALU.add))
        v(lambda: ve.tensor_tensor(pr[:, :, 3:5], c4[:, :, 1:2].broadcast_to([P, 16, 2]), c4[:, :, 2:4], ALU.add))
        v(lambda: ve.tensor_tensor(pr[:, :, 5:6], c4[:, :, 2:3], c4[:, :, 3:4], ALU.add))
        v(lambda: ve.tensor_reduce(grp, pr, AX.X, ALU.max))

        def ranked(val, n, rows, low, gt, ge, out_, keep):
            vv = val.rearrange("p (r i) -> p r i", i=n)
            other = vv.unsqueeze(2).broadcast_to([P, rows, n, n])
            mine = vv.unsqueeze(3).broadcast_to([P, rows, n, n])
            g4 = gt.rearrange("p (r i j) -> p r i j", r=rows, i=n)
            e4 = ge.rearrange("p (r i j) -> p r i j", r=rows, i=n)
            g3 = gt.rearrange("p (r c) -> p r c", r=rows)
            e3 = ge.rearrange("p (r c) -> p r c", r=rows)
            lw = low.unsqueeze(1).broadcast_to([P, rows, n * n])
            v(lambda: ve.tensor_tensor(g4, other, mine, ALU.is_gt))
            v(lambda: ve.tensor_tensor(e4, other, mine, ALU.is_equal))
            v(lambda: ve.tensor_tensor(e3, e3, lw, ALU.mult))
            v(lambda: ve.tensor_tensor(gt, gt, ge, ALU.add))
            v(lambda: ve.tensor_reduce(out_, g4, AX.X, ALU.add))
            v(lambda: ve.tensor_scalar(out_, out_, float(keep), None, ALU.is_lt))

        vi(lambda: ve.memset(small[:, 50:51], 0.0), "lowok", ("d.low",))
        ranked(grp, 4, NT, lowt[:, 0:16], s1[:, 0:64], s1[:, 64:128], gsel, 2)
        g3 = gsel.unsqueeze(2).broadcast_to([P, 16, 4])
        m3 = mch.rearrange("p (g i) -> p g i", i=4)
        v(lambda: ve.tensor_tensor(m3, c4, g3, ALU.mult))
        v(lambda: ve.tensor_scalar(gsel, gsel, 1.0, 1e9, ALU.subtract, ALU.mult))
        v(lambda: ve.tensor_tensor(m3, m3, g3, ALU.add))
        ranked(mch, E, NT, lowt[:, 16:272], s2, s3, msel, 4)
        sel0 = selc[:, 4, :]
        m3e = msel.rearrange("p (m e) -> p m e", m=NT)
        v(lambda: ve.memset(selc[:, 0, :], 0.0), None, ("p.y3", "p.bu3", "v.xs3"))
        for m in range(NT):
            v(lambda m=m: ve.tensor_tensor(selc[:, m + 1, :], selc[:, m, :], m3e[:, m, :], ALU.add),
              "selc" if m == NT - 1 else None)
        def weights(e):
            w = wbufs[e % NW]
            return w[:, 0:2048].rearrange("p (k n) -> p k n", k=KC), w[:, 2048:3072].rearrange("p (i n) -> p i n", i=2)

        A.do(lambda: ae.activation(xh.rearrange("p m d -> p (m d)"), xn3.rearrange("p m d -> p (m d)"), ACT.Copy),
             "xh", ("v.l3.xn3", "p.y3"))
        v(lambda: ve.tensor_tensor(xl.rearrange("p m d -> p (m d)"), xn3.rearrange("p m d -> p (m d)"),
                                   xh.rearrange("p m d -> p (m d)"), ALU.subtract), "xl", ("a.xh", "p.y3"))
        gu0, dn0 = weights(0)
        for i in range(4):
            product(bank(i), lambda k, i=i: gu0[:, k, i * P:(i + 1) * P], lambda k: xt3[:, k, :], KC, f"gu0.{i}",
                    ("d.wgu0",), each=by_chunk("l3"))
        A.do(lambda: ae.activation(silu0, psum[:, 0:2, :].rearrange("p a n -> p (a n)"), ACT.Silu), "si0",
             ("p.gu0.1", "p.y3"))
        for i in range(2):
            vi(lambda i=i: ve.tensor_tensor(hid0[:, i, :], silu0[:, i * T:(i + 1) * T], bank(2 + i), ALU.mult), f"h0.{i}",
               ("a.si0", f"p.gu0.{2 + i}"))
        PE.do(lambda: pe.matmul(psum[:, 4, 64:128], ltri, msel, start=True, stop=False), None, ("v.selc", "d.ltri"))
        PE.do(lambda: pe.matmul(psum[:, 4, 64:128], ones[:, :], selc[:, 0:4, :].rearrange("p m e -> p (m e)"),
                                start=False, stop=True))
        PE.do(lambda: pe.matmul(psum[:, 5, 0:E], ones[:, :], sel0, start=True, stop=True), "before")
        v(lambda: ve.scalar_tensor_tensor(out=posm, in0=psum[:, 4, 64:128], scalar=1.0, in1=msel, op0=ALU.add,
                                          op1=ALU.mult), None, ("p.before",))
        v(lambda: ve.tensor_scalar(posm, posm, -1.0, None, ALU.add), "pos")
        v(lambda: ve.tensor_copy(cnt[0:1, :], psum[0:1, 5, 0:E]), "cnt")
        vi(lambda: pick(picks[2], 0, 0), "pick0", ("d.iota", "v.pos"))
        V.do(lambda: ve.sem_inc(v_first, 1), wait=("v.pick0",))
        ready = ("v.cnt",)
        SP.do(prepare(sp, "s"), wait=ready)
        GP.do(prepare(gp, "g", [g_sum]), wait=ready)
        v(lambda: ve.tensor_tensor(msel, msel, scr, ALU.mult))
        v(lambda: ve.tensor_reduce(wsum, msel.rearrange("p (m e) -> p m e", m=NT), AX.X, ALU.add))
        v(lambda: ve.tensor_scalar(wsum, wsum, 1e-20, None, ALU.add))
        v(lambda: ve.reciprocal(wsum, wsum))
        v(lambda: ve.tensor_scalar(wsum, wsum, 2.5, None, ALU.mult))
        v(lambda: ve.tensor_tensor(comb[:, :, :], m3e, wsum.unsqueeze(2).broadcast_to([P, NT, E]), ALU.mult), "comb")
        v(lambda: ve.memset(rh[:, :, :, 3:4], 0.0))
        v(lambda: ve.memset(hid, 0.0))
        v(lambda: ve.tensor_copy(rh[:, :, :, 0], tokc[:, 0:NT].unsqueeze(2).broadcast_to([P, NT, E])), None,
          ("d.tokc",))
        v(lambda: ve.tensor_copy(rh[:, :, :, 1], comb[:, :, :]))
        v(lambda: ve.tensor_tensor(rh[:, :, :, 2], comb[:, :, :], rh[:, :, :, 1], ALU.subtract), "rh")
        V.do(prepare(ve, "v", [v_pick, v_list, v_pad, v_rows, v_xg, v_hid]), wait=ready)
        A.do(prepare(ae, "a", [a_xg, a_silu, a_turn, a_y]), wait=ready)
        for m in range(NT):
            if m == 2:
                PE.do(prepare(pe, "p", [p_lo, p_hi, p_list, p_turn, p_gate, p_down]), wait=ready)
            product(bank((6, 7, 4, 6)[m]), lambda k, m=m: hid0[:, k, m * P:(m + 1) * P], lambda k: dn0[:, k, :], 2,
                    f"gd0.{m}", ("d.wdn0", "a.scr") + (("v.cnt",) if m == 2 else ("v.x3.0",) if m == 3 else ()),
                    each=lambda k: f"v.h0.{k}")
            vi(lambda m=m: ve.scalar_tensor_tensor(out=xr[:, m, :], in0=bank((6, 7, 4, 6)[m]),
                                                   scalar=comb[:, m, 0:1], in1=xr[:, m, :], op0=ALU.mult,
                                                   op1=ALU.add), f"x3.{m}", (f"p.gd0.{m}", "v.comb"))

        def tiles(eng, tile, halves=False, empty=None, tail=None, start=None, end=None):
            def run():
                c = counts[eng]

                def before(n, fn):
                    if n:
                        with eng.If(c[n - 1] > 0):
                            fn()

                for n in range(NE):
                    if start:
                        start(n)

                    def level(i):
                        if i == NT:
                            if tail:
                                tail(n, NT - 1)
                            return
                        with eng.If(c[n] > P * i):
                            if halves:
                                with eng.If(c[n] > P * i + HALF):
                                    tile(n, i, before, P)
                                with eng.Else():
                                    tile(n, i, before, HALF)
                            else:
                                tile(n, i, before)
                            eng.reg_add(now[eng], now[eng], 1)
                            eng.reg_add(this[eng], this[eng], 1)
                            level(i + 1)
                        if i and tail:
                            with eng.Else():
                                tail(n, i - 1)
                        if not i and empty:
                            with eng.Else():
                                empty(n, before)
                    level(0)
                if end:
                    before(NE, end)
            return run

        def pe_turn():
            pe.wait_ge(v_hid, now[pe])
            for c in range(2):
                tr = pe.transpose(psum[:, 2, c * P:(c + 1) * P], hid[:, c * P:(c + 1) * P], ident[:, :])
            tr.then_inc(p_turn, 1)

        def pe_down(n):
            dn = weights(n + 1)[1]
            pe.wait_ge(dsem[f"wdn{n + 1}"], 16)
            pe.wait_ge(a_turn, now[pe])
            for c in range(2):
                mm = pe.matmul(bank(4), hidt[:, c * P:(c + 1) * P], dn[:, c, :], start=(c == 0), stop=(c == 1))
            mm.then_inc(p_down, 1)

        def pe_both(n):
            pe_turn()
            pe_down(n)

        def pe_tile(n, i, before, size):
            if i:
                pk = picks[i % 2]
                pe.wait_ge(v_pick, now[pe])
            else:
                pk = picks[2 + n % 2]
                pe.wait_ge(v_first, n + 1)
            pe.wait_ge(v_xg, now[pe])
            pe.wait_ge(a_xg, now[pe])
            for k in range(KC):
                for j, part_ in enumerate((xh, xl)):
                    for m in range(NT):
                        mm = pe.matmul(psum[:, 5 * (k // 2), (k % 2) * P:(k % 2) * P + size],
                                       part_[:, m, k * P:(k + 1) * P], pk[:, m, 0:size],
                                       start=(j == 0 and m == 0), stop=(j == 1 and m == NT - 1))
                if k % 2:
                    mm.then_inc(p_hi if k == 3 else p_lo, 1)
            pe.wait_ge(v_list, now[pe])
            for m in range(NT):
                mm = pe.matmul(psum[:, 1, 0:4], pk[:, m, :], rh[:, m, n + 1, :], start=(m == 0), stop=(m == NT - 1))
            mm.then_inc(p_list, 1)
            if i:
                pe_turn()
            else:
                before(n, pe_turn)
            gu, _ = weights(n + 1)
            pe.wait_ge(dsem[f"wgu{n + 1}"], 16)
            pe.wait_ge(a_xg, this[pe])
            for k in range(KC):
                if k == 2:
                    pe.wait_ge(v_xg, this[pe])
                if size == P:
                    mm = pe.matmul(bank(3), xg[:, k * P:(k + 1) * P], gu[:, k, :], start=(k == 0), stop=(k == KC - 1))
                else:
                    for o in range(2):
                        mm = pe.matmul(psum[HALF * (1 - o):HALF * (2 - o), 3, I * o:I * o + I],
                                       xg[:, k * P:k * P + HALF], gu[:, k, I * o:I * o + I], start=(k == 0),
                                       stop=(k == KC - 1))
            mm.then_inc(p_gate, 1)
            if i:
                pe_down(n)
            else:
                before(n, lambda: pe_down(n - 1))

        def pick_first(n):
            if n < NE:
                ve.wait_ge(v_first, n)
                pick(picks[2 + n % 2], n, 0).then_inc(v_first, 1)

        def slots(ap, size):
            return ap.rearrange("p (k s) -> p k s", k=2)[:, :, 0:size]

        def v_tile(n, i, before, size):
            ve.wait_ge(p_hi, this[ve])
            ve.wait_ge(p_gate, now[ve])
            ve.tensor_copy(slots(xg[:, 256:512], size), slots(psum[:, 5, 0:256], size)).then_inc(v_xg, 1)
            ve.wait_ge(p_list, this[ve])
            ve.wait_ge(v_rows, now[ve])
            ve.tensor_copy(lst, psum[:, 1, 0:4]).then_inc(v_list, 1)
            ve.wait_ge(v_list, this[ve])
            ve.wait_ge(v_hid, now[ve])
            ve.tensor_tensor(wcol, lst[:, 1:2], lst[:, 2:3], ALU.add)
            ve.tensor_scalar(pad, lst[:, 0:1], 0.0, tokc[:, 4:5], ALU.is_equal, ALU.mult).then_inc(v_pad, 1)
            if i == 0:
                pick_first(n + 1)
            ve.wait_ge(v_pad, this[ve])
            t = NT * n + i
            ve.scalar_tensor_tensor(out=slot_rows[:, t:t + 1], in0=lst[:, 0:1], scalar=-1.0, in1=pad, op0=ALU.add,
                                    op1=ALU.add).then_inc(v_rows, 1)
            if i < NT - 1:
                ve.wait_ge(v_pick, now[ve])
                pick(picks[(i + 1) % 2], n, i + 1).then_inc(v_pick, 1)
            else:
                ve.wait_ge(v_pick, now[ve])
                ve.sem_inc(v_pick, 1)
            ve.wait_ge(a_silu, this[ve])
            ve.wait_ge(p_turn, now[ve])
            ve.scalar_tensor_tensor(out=hid[0:size, :], in0=silu[0:size, :], scalar=wcol[0:size, :],
                                    in1=psum[0:size, 3, 256:512], op0=ALU.mult, op1=ALU.mult).then_inc(v_hid, 1)

        def v_empty(n, before):
            if n + 1 < NE:
                ve.wait_ge(p_list, now[ve])
                pick_first(n + 1)

        def a_turned():
            ae.wait_ge(p_turn, now[ae])
            ae.activation(hidt, psum[:, 2, 0:256], ACT.Copy).then_inc(a_turn, 1)

        def a_down(n, i):
            ae.wait_ge(p_down, now[ae])
            if i == 0:
                y, ready = ys[6 + (n - 1) % 4], base4
            else:
                y, ready = ys[3 * (n % 2) + i - 1], base1
            ae.wait_ge(g_sum, ready[ae])
            ae.activation(y, bank(4), ACT.Copy).then_inc(a_y, 1)

        def a_both(n):
            a_turned()
            a_down(n + 1, 0)

        a_at = {}

        def a_start(n):
            if n == 0:
                a_at[0] = ae.alloc_register("a_at")
                ae.reg_mov(a_at[0], 1)
            ae.reg_mov(base4[ae], base3[ae])
            ae.reg_mov(base3[ae], base2[ae])
            ae.reg_mov(base2[ae], base1[ae])
            ae.reg_mov(base1[ae], a_at[0])
            ae.reg_mov(a_at[0], now[ae])

        def a_tile(n, i, before, size):
            ae.wait_ge(p_lo, this[ae])
            ae.wait_ge(p_gate, now[ae])
            ae.activation(slots(xg[:, 0:256], size), slots(psum[:, 0, 0:256], size), ACT.Copy).then_inc(a_xg, 1)
            if i:
                a_turned()
            else:
                before(n, a_turned)
            ae.wait_ge(p_gate, this[ae])
            ae.wait_ge(v_hid, now[ae])
            ae.activation(silu[0:size, :], psum[P - size:P, 3, 0:256], ACT.Silu).then_inc(a_silu, 1)
            if i:
                a_down(n, i)
            else:
                before(n, lambda: a_down(n, 0))

        def g_scatter(y, n, i):
            j = NT * n + i
            gp.sem_inc(g_turn, 1)
            gp.indirect_dma_start(out, bass.IndirectOffsetOnAxis(slot_rows[:, j:j + 1].bitcast(mybir.dt.uint32), 0),
                                  y, None, bounds_check=T + P - 1, oob_is_err=True,
                                  compute_op=ALU.add).then_inc(g_dma, 16)
            gp.wait_ge(g_dma, now16[gp])
            gp.sem_inc(g_sum, 1)
            gp.reg_add(now16[gp], now16[gp], 16)

        def g_tile(n, i, before):
            if i:
                gp.wait_ge(a_y, now[gp])
                gp.wait_ge(v_rows, now[gp])
                g_scatter(ys[3 * (n % 2) + i - 1], n, i - 1)

        def g_tail(n, last):
            gp.wait_ge(a_y, now[gp])
            gp.wait_ge(v_rows, now[gp])
            g_scatter(ys[6 + n % 4], n, last)

        for m in range(NT):
            SP.do(lambda m=m: sp.dma_start(out.rearrange("(m p) d -> p m d", p=P)[:, m, :], xr[:, m, :])
                  .then_inc(s_out, 16), wait=(f"v.x3.{m}",))
        SP.do(lambda: sp.dma_start(out.rearrange("(m p) d -> p m d", p=P)[:, NT, :], xr[:, 0, :])
              .then_inc(s_out, 16))
        def load_weights(e, wait=()):
            w = wbufs[e % NW]
            load(f"wgu{e}", w[:, 0:2048].rearrange("p (k n) -> p k n", k=KC), io["wgu"][e], wait)
            load(f"wdn{e}", w[:, 2048:3072].rearrange("p (i n) -> p i n", i=2), io["wdn"][e], wait)

        load_weights(NW, ("p.gd0.3",))
        for e in range(NW + 1, E):
            for name in ("wgu", "wdn"):
                dsem[f"{name}{e}"] = sem(f"d_{name}{e}")

        def s_start(n):
            e = n + NW
            if n and e < E:
                w = wbufs[e % NW]
                sp.wait_ge(p_down, now[sp])
                sp.wait_ge(dsem[f"wgu{n}"], 16)
                sp.wait_ge(dsem[f"wdn{n}"], 16)
                sp.dma_start(w[:, 0:2048].rearrange("p (k n) -> p k n", k=KC), io["wgu"][e]).then_inc(
                    dsem[f"wgu{e}"], 16)
                sp.dma_start(w[:, 2048:3072].rearrange("p (i n) -> p i n", i=2), io["wdn"][e]).then_inc(
                    dsem[f"wdn{e}"], 16)


        V.do(tiles(ve, v_tile, halves=True, empty=v_empty))
        A.do(tiles(ae, a_tile, halves=True, empty=lambda n, before: before(n, lambda: a_both(n - 1)), start=a_start,
                   end=lambda: a_both(NE - 1)), wait=("v.pick0", "v.xl", "v.rh"))
        PE.do(tiles(pe, pe_tile, halves=True, empty=lambda n, before: before(n, lambda: pe_both(n - 1)),
                    end=lambda: pe_both(NE - 1)), wait=("v.pick0", "v.xl", "v.x3.2", "v.rh"))
        GP.do(lambda: gp.wait_ge(s_out, 16 * (NT + 1)))
        GP.do(tiles(gp, g_tile, tail=g_tail))
        GP.do(lambda: gp.sem_inc(g_end, 1))
        SP.do(tiles(sp, lambda n, i, before: None, start=s_start))
        SP.do(lambda: sp.wait_ge(s_out, 16 * (NT + 1)))
        SP.do(lambda: sp.wait_ge(g_end, 1))
        SP.do(lambda: None, wait=[f"d.{w}{e}" for e in range(E - NW, E) for w in ("wgu", "wdn")])

        block = ctx.enter_context(nc.Block())

        @block.sync
        def _(eng):
            emit(SP, eng, Q, dsem)

        @block.vector
        def _(eng):
            emit(V, eng, Q, dsem)

        @block.scalar
        def _(eng):
            emit(A, eng, Q, dsem)

        @block.tensor
        def _(eng):
            emit(PE, eng, Q, dsem)

        @block.gpsimd
        def _(eng):
            emit(GP, eng, Q, dsem)


def laid_out(a):
    def kt(w):
        return np.ascontiguousarray(w.T.reshape(KC, P, w.shape[0]).transpose(1, 0, 2))

    f = np.float32
    c = a["ctx_1024"]
    ring = np.zeros((B, NB * P, D), c.dtype)
    ring[:, 0:DEAD] = c[:, M - DEAD:]
    ring[:, DEAD + 1:M + 1] = c[:, :M - DEAD]
    ctx = ring.reshape(B, NB, P, KC, P).transpose(1, 4, 0, 3, 2)
    mask = np.zeros((B, P * 13), a["mask_BxS2_if0"].dtype)
    mask[:, :M] = a["mask_BxS2_if0"]
    wk, wv = a["L0_xattn_Wk"], a["L0_xattn_Wv"]
    order = np.stack([np.arange(D).reshape(H, HD), D + np.arange(D).reshape(H, HD)], 1)
    odd = np.arange(H) // 2 % 2 == 1
    order[odd] = order[odd][:, ::-1]
    order = order.ravel()
    wkv = np.concatenate([wk, wv])[order]
    bkv = np.concatenate([a["L0_xattn_bk"], a["L0_xattn_bv"]])[order][None]
    woff = np.zeros((2, 104, D), f)
    boff = np.zeros((2, 104), f)
    ref = np.zeros((2, 104), f)
    for g in range(2):
        for o in (0, 64):
            woff[g, o:o + 40] = a["L0_xattn_Woff"][40 * g:40 * g + 40]
            boff[g, o:o + 40] = a["L0_xattn_boff"][40 * g:40 * g + 40]
            ref[g, o:o + 40] = np.tile(np.arange(NK) - 3, 8)
    cols = np.zeros((P, C_N), f)
    cols[0:104, C_BOFF:C_BOFF + 2] = boff.T
    cols[0:104, C_REF:C_REF + 2] = ref.T
    cols[:, C_BQ:C_BQ + 4] = a["L0_xattn_bq"].reshape(4, P).T
    cols[:, C_BB:C_BB + 4] = a["L0_attn_b_B"].reshape(4, P).T
    cols[:, C_LOGA:C_LOGA + 4] = a["L0_attn_log_A"].reshape(4, P).T
    cols[:, C_DT] = a["L0_attn_log_dt"][0]
    p = np.arange(P)
    row = np.arange(NB * P).reshape(NB, P, 1)
    vld = ((row != DEAD) & (row <= M)).astype(f)
    cols[:, C_VLD] = vld[0, :, 0]
    cols[:, C_NEGP] = 64 - p
    sel = np.zeros((104, 40), np.float16)
    sel[np.arange(40), np.arange(40)] = 1
    sel[64 + np.arange(40), np.arange(40)] = 1
    zsel = np.zeros((P, 2, 126), f)
    for o in range(2):
        zsel[32 * o:32 * o + 32, o, 62] = 1
        zsel[64 + 32 * o:96 + 32 * o, o, 63] = 1
    bsel = np.zeros((P, 32, P), np.float16)
    wo = np.zeros((P, 4, D), f)
    wot = a["L0_xattn_Wo"].T.reshape(4, 4, HD, D)
    for i, at in enumerate((32, 96, 0, 64)):
        wo[at:at + 32] = wot[:, i].transpose(1, 0, 2)
        for w in range(32):
            bsel[64 * (i // 2) + 2 * w + i % 2, w, at:at + 32] = 1
    low4 = (np.arange(4)[None, :] < np.arange(4)[:, None]).astype(f)
    low16 = (np.arange(16)[None, :] < np.arange(16)[:, None]).astype(f)
    wg, wu = a["L0_ffn_w_gate"], a["L0_ffn_w_up"]
    wgu = np.concatenate([wg, wu], 1).transpose(0, 2, 1).reshape(E, KC, P, 2 * I).transpose(0, 2, 1, 3)
    wdn = a["L0_ffn_w_down"].transpose(0, 2, 1).reshape(E, 2, P, D).transpose(0, 2, 1, 3)
    return {
        "x": a["x"].reshape(T, D), "ctx": ctx, "mask": mask.reshape(B, P, 13).transpose(1, 0, 2), "wkv": kt(wkv),
        "bkv": bkv, "wq": kt(a["L0_xattn_Wq"]),
        "woff": woff.transpose(2, 0, 1).reshape(KC, P, 2, 104).transpose(1, 0, 2, 3), "cols": cols,
        "loc": np.tile(np.arange(S), B).astype(f)[None], "sel": sel, "zsel": zsel, "bsel": bsel,
        "ident": np.eye(P, dtype=f), "vld": vld, "wo": wo,
        "rows": np.stack([a["L0_xattn_bo"], a["L0_attn_b_C"], a["L0_attn_b_D"]]), "wb": kt(a["L0_attn_W_B"]),
        "wc": kt(a["L0_attn_W_C"]), "wd": kt(a["L0_attn_W_D"]), "rw": kt(a["L0_ffn_router_weight"]),
        "rb": a["L0_ffn_router_bias"][None], "low": np.concatenate([low4.ravel(), low16.ravel()])[None],
        "ltri": (p[:, None] < p[None, :]).astype(f), "iota": np.arange(T).astype(np.float16)[None],
        "tokc": np.concatenate([p[:, None] + P * np.arange(NT)[None] + 1, p[:, None] + T + 1], 1).astype(f),
        "wgu": wgu, "wdn": wdn,
    }


def kernel(**inputs):
    import concourse.bacc as _bacc
    from concourse import mybir as _mybir
    from concourse.bass_utils import run_bass_kernel_spmd as _run

    nc = _bacc.Bacc("TRN2", target_bir_lowering=False, num_devices=1)
    data = laid_out({k: np.asarray(v) for k, v in inputs.items()})
    arrays, io = {}, {}
    for name, shape, dt in INPUTS:
        a = np.ascontiguousarray(data[name])
        assert a.shape == shape, (name, a.shape)
        arrays[f"in_{name}"] = a
        io[name] = nc.dram_tensor(f"in_{name}", shape, dt, kind="ExternalInput").ap()
    out = nc.dram_tensor("out_0", (T + P, D), F32, kind="ExternalOutput").ap()
    program(nc, io, out)
    r = _run(nc, [arrays], core_ids=[0])
    return r.results[0]["out_0"][0:T].reshape(B, S, D)
```
